# Optimizing a Trainium2 kernel written in Bass

```python
import numpy as np
import jax
import jax.numpy as jnp

def _softmax(x, axis=-1):
    return jax.nn.softmax(x, axis=axis)

def _gelu(x):
    return jax.nn.gelu(x, approximate=True)

def _silu(x):
    return jax.nn.silu(x)

def _sigmoid(x):
    return jax.nn.sigmoid(x)

def _layernorm(x, axis=-1, eps=1e-05):
    m = jnp.mean(x, axis=axis, keepdims=True)
    v = jnp.var(x, axis=axis, keepdims=True)
    return (x - m) / jnp.sqrt(v + eps)

def _scatter_add(tgt, idx, src, axis=0):
    return tgt.at[idx].add(src)

def _segment_sum(src, seg, n):
    return jax.ops.segment_sum(src, seg, n)
kernel_name = 'mk_macaron_d4_jaxref_r8_44bd70'

def setup_inputs(seed: int=0):
    np.random.seed(seed)
    _w = jnp.asarray

    def _L0_attn_setup():
        import jax, jax.numpy as jnp
        import numpy as np
        THETA = 10000.0

        def _rope_tables(seq_len, head_dim):
            dims = jnp.arange(0, head_dim, 2, dtype=jnp.float32)
            inv_freq = 1.0 / THETA ** (dims / head_dim)
            angles = jnp.arange(seq_len, dtype=jnp.float32)[:, None] * inv_freq[None, :]
            return (jnp.cos(angles), jnp.sin(angles))

        def _apply_rope(x, cos, sin):
            B, H, S, hd = x.shape
            xp = x.reshape(B, H, S, hd // 2, 2)
            x0, x1 = (xp[..., 0], xp[..., 1])
            c = cos[None, None, :, :]
            s = sin[None, None, :, :]
            r0 = x0 * c - x1 * s
            r1 = x0 * s + x1 * c
            return jnp.stack([r0, r1], axis=-1).reshape(B, H, S, hd)
        key = jax.random.key(seed)
        k1, k2, k3, k4, k5 = jax.random.split(key, 5)
        B, S, D = (2, 256, 128)
        x = jax.random.normal(k1, (B, S, D), dtype=jnp.float32)
        w_qkv = jax.random.normal(k2, (3 * D, D), dtype=jnp.float32) * (1.0 / np.sqrt(D))
        b_qkv = jax.random.normal(k3, (3 * D,), dtype=jnp.float32) * 0.02
        w_out = jax.random.normal(k4, (D, D), dtype=jnp.float32) * (1.0 / np.sqrt(D))
        b_out = jax.random.normal(k5, (D,), dtype=jnp.float32) * 0.02
        return {'x': x, 'w_qkv': w_qkv, 'b_qkv': b_qkv, 'w_out': w_out, 'b_out': b_out}
    _L0_attn_in = _L0_attn_setup()

    def _L0_ffn_setup():
        import jax, jax.numpy as jnp
        import numpy as np
        D_IN, D_HID = (128, 512)

        def _ternary(key, shape):
            return jax.random.randint(key, shape, -1, 2).astype(jnp.float32)

        def _tlin(x, w, s):
            return jnp.einsum('bsi,oi->bso', x, w) * s
        key = jax.random.key(seed)
        ks = jax.random.split(key, 12)
        inv = lambda fan: 1.0 / np.sqrt(fan).astype(np.float32)
        return {'x': jax.random.normal(ks[0], (4, 256, D_IN), dtype=jnp.float32), 'w1_w': _ternary(ks[1], (D_HID, D_IN)), 'w1_s': jax.random.uniform(ks[2], (D_HID,), dtype=jnp.float32) * inv(D_IN), 'w2_w': _ternary(ks[3], (D_HID, D_IN)), 'w2_s': jax.random.uniform(ks[4], (D_HID,), dtype=jnp.float32) * inv(D_IN), 'h1_w': _ternary(ks[5], (D_HID, D_HID)), 'h1_s': jax.random.uniform(ks[6], (D_HID,), dtype=jnp.float32) * inv(D_HID), 'h2_w': _ternary(ks[7], (D_HID, D_HID)), 'h2_s': jax.random.uniform(ks[8], (D_HID,), dtype=jnp.float32) * inv(D_HID), 'w3_w': _ternary(ks[9], (D_IN, D_HID)), 'w3_s': jax.random.uniform(ks[10], (D_IN,), dtype=jnp.float32) * inv(D_HID)}
    _L0_ffn_in = _L0_ffn_setup()

    def _L1_attn_setup():
        import jax, jax.numpy as jnp
        import numpy as np
        from jax import lax
        key = jax.random.key(seed)
        ks = jax.random.split(key, 9)
        B, L, d_model = (1, 256, 128)
        d_inner, d_state, d_conv = (256, 16, 4)

        def g(k, shape, scale):
            return jax.random.normal(k, shape, dtype=jnp.float32) * scale
        return dict(x=g(ks[0], (B, L, d_model), 1.0), in_proj_w=g(ks[1], (2 * d_inner, d_model), 0.02), conv_w=g(ks[2], (d_inner, 1, d_conv), 0.1), conv_b=g(ks[3], (d_inner,), 0.02), x_proj_w=g(ks[4], (2 * d_state, d_inner), 0.02), dt_proj_w=g(ks[5], (d_inner, d_inner), 0.02), dt_proj_b=g(ks[6], (d_inner,), 0.02), out_proj_w=g(ks[7], (d_model, d_inner), 0.02), A_log=jnp.log(jnp.arange(1, d_state + 1, dtype=jnp.float32)), D_param=jnp.ones((d_inner,), dtype=jnp.float32))
    _L1_attn_in = _L1_attn_setup()

    def _L1_ffn_setup():
        import jax, jax.numpy as jnp
        import numpy as np
        B, S, D, O, E, K = (2, 256, 128, 128, 8, 2)
        key = jax.random.key(seed)
        ks = jax.random.split(key, 6)

        def w(k, shape, fan_in):
            return jax.random.normal(k, shape, jnp.float32) * fan_in ** (-0.5)
        return {'x': jax.random.normal(ks[0], (B, S, D), jnp.float32), 'gate_w': w(ks[1], (E, D), D), 'gate_b': jnp.zeros((E,), jnp.float32), 'w1': w(ks[2], (E, D, O), D), 'b1': jnp.zeros((E, O), jnp.float32), 'w2': w(ks[3], (E, O, O), O), 'b2': jnp.zeros((E, O), jnp.float32), 'w3': w(ks[4], (E, O, O), O), 'b3': jnp.zeros((E, O), jnp.float32)}
    _L1_ffn_in = _L1_ffn_setup()

    def _L2_attn_setup():
        import jax, jax.numpy as jnp
        import numpy as np
        from jax import lax
        D_MODEL = 128
        D_IN = 128
        N_STATE = 16
        DT_RANK = 64
        D_FFN = 512
        BATCH, SEQ = (2, 256)

        def _ln(x, g, b, eps=1e-05):
            m = x.mean(-1, keepdims=True)
            v = ((x - m) ** 2).mean(-1, keepdims=True)
            return (x - m) / jnp.sqrt(v + eps) * g + b

        def _mamba(x, in_proj_w, conv_w, conv_b, x_proj_w, dt_proj_w, dt_proj_b, A_log, Dp, out_proj_w):
            B, L, _ = x.shape
            xz = x @ in_proj_w.T
            x_in, z = jnp.split(xz, 2, axis=-1)
            x_prev = jnp.pad(x_in, ((0, 0), (1, 0), (0, 0)))[:, :L]
            x_c = jax.nn.silu(x_prev * conv_w[:, 0] + x_in * conv_w[:, 1] + conv_b)
            x_dbl = x_c @ x_proj_w.T
            dt, Bm, Cm = jnp.split(x_dbl, [DT_RANK, DT_RANK + N_STATE], axis=-1)
            delta = jax.nn.softplus(dt @ dt_proj_w.T + dt_proj_b)
            A = -jnp.exp(A_log)
            deltaA = jnp.exp(delta[..., None] * A)
            dBu = delta[..., None] * Bm[:, :, None, :] * x_c[..., None]

            def step(h, t):
                dA_t, dBu_t, C_t = t
                h = dA_t * h + dBu_t
                y = jnp.einsum('bdn,bn->bd', h, C_t)
                return (h, y)
            h0 = jnp.zeros((B, D_IN, N_STATE), x.dtype)
            _, ys = lax.scan(step, h0, (deltaA.transpose(1, 0, 2, 3), dBu.transpose(1, 0, 2, 3), Cm.transpose(1, 0, 2)))
            y = ys.transpose(1, 0, 2)
            y = (y + x_c * Dp) * jax.nn.silu(z)
            return y @ out_proj_w.T
        key = jax.random.key(seed)
        ks = jax.random.split(key, 12)
        r = lambda i, shape, s=0.02: jax.random.normal(ks[i], shape, jnp.float32) * s
        ones = lambda n: jnp.ones((n,), jnp.float32)
        zeros = lambda n: jnp.zeros((n,), jnp.float32)
        A_log = jnp.log(jnp.tile(jnp.arange(1, N_STATE + 1, dtype=jnp.float32), (D_IN, 1)))
        return {'src': jax.random.normal(ks[0], (BATCH, SEQ, D_MODEL), jnp.float32), 'in_proj_w': r(1, (2 * D_IN, D_MODEL)), 'conv_w': r(2, (D_IN, 2), 0.5), 'conv_b': zeros(D_IN), 'x_proj_w': r(3, (DT_RANK + 2 * N_STATE, D_IN)), 'dt_proj_w': r(4, (D_IN, DT_RANK), 0.1), 'dt_proj_b': r(5, (D_IN,), 0.1), 'A_log': A_log, 'Dp': ones(D_IN), 'out_proj_w': r(6, (D_MODEL, D_IN)), 'mnorm_g': ones(D_MODEL), 'mnorm_b': zeros(D_MODEL), 'n1_g': ones(D_MODEL), 'n1_b': zeros(D_MODEL), 'n2_g': ones(D_MODEL), 'n2_b': zeros(D_MODEL), 'n3_g': ones(D_MODEL), 'n3_b': zeros(D_MODEL), 'ffn_w1': r(7, (D_FFN, D_MODEL)), 'ffn_w2': r(8, (D_MODEL, D_FFN)), 'fe_w': r(9, (D_MODEL, D_MODEL)), 'fe_b': zeros(D_MODEL)}
    _L2_attn_in = _L2_attn_setup()

    def _L2_ffn_setup():
        import jax, jax.numpy as jnp
        import numpy as np
        D = 128
        F = 128
        E = 8
        K = 2
        B, T = (2, 256)

        def _moe_forward(x, router_w, w1, w2, shared_gate_up, shared_down, shared_gate_w):
            b, t, d = x.shape
            xf = x.reshape(-1, d)
            n = xf.shape[0]
            logits = xf @ router_w
            probs = jax.nn.softmax(logits, axis=-1)
            topw, topi = jax.lax.top_k(probs, K)
            combine = jnp.zeros((n, E), dtype=probs.dtype).at[jnp.arange(n)[:, None], topi].add(topw)
            h = jax.nn.silu(jnp.einsum('nd,edf->nef', xf, w1))
            ye = jnp.einsum('nef,efd->ned', h, w2)
            routed = jnp.einsum('ne,ned->nd', combine, ye)
            gu = xf @ shared_gate_up
            gate, up = (gu[:, :F], gu[:, F:])
            shared = jax.nn.silu(gate) * up @ shared_down
            shared = jax.nn.sigmoid(xf @ shared_gate_w) * shared
            return (routed + shared).reshape(b, t, d)
        key = jax.random.key(seed)
        ks = jax.random.split(key, 7)
        std = 0.02
        x = jax.random.normal(ks[0], (B, T, D), dtype=jnp.float32)
        router_w = jax.random.normal(ks[1], (D, E), dtype=jnp.float32) * std
        w1 = jax.random.normal(ks[2], (E, D, F), dtype=jnp.float32) * std
        w2 = jax.random.normal(ks[3], (E, F, D), dtype=jnp.float32) * std
        shared_gate_up = jax.random.normal(ks[4], (D, 2 * F), dtype=jnp.float32) * std
        shared_down = jax.random.normal(ks[5], (F, D), dtype=jnp.float32) * std
        shared_gate_w = jax.random.normal(ks[6], (D, 1), dtype=jnp.float32) * std
        return {'x': x, 'router_w': router_w, 'w1': w1, 'w2': w2, 'shared_gate_up': shared_gate_up, 'shared_down': shared_down, 'shared_gate_w': shared_gate_w}
    _L2_ffn_in = _L2_ffn_setup()

    def _L3_attn_setup():
        import jax, jax.numpy as jnp
        import numpy as np
        DIM = 128
        HEADS = 16
        HEAD_DIM = DIM // HEADS
        B, S = (4, 512)
        key = jax.random.key(seed)
        ks = jax.random.split(key, 8)
        sc = 1.0 / np.sqrt(DIM)
        return {'x': jax.random.normal(ks[0], (B, S, DIM), dtype=jnp.float32), 'Wq': jax.random.normal(ks[1], (DIM, DIM), dtype=jnp.float32) * sc, 'Wk': jax.random.normal(ks[2], (DIM, DIM), dtype=jnp.float32) * sc, 'Wv': jax.random.normal(ks[3], (DIM, DIM), dtype=jnp.float32) * sc, 'Wp': jax.random.normal(ks[4], (DIM, DIM), dtype=jnp.float32) * sc, 'bp': jnp.zeros((DIM,), dtype=jnp.float32), 'conv_w': jax.random.normal(ks[5], (DIM, 3), dtype=jnp.float32) * (1.0 / np.sqrt(3.0)), 'conv_b': jnp.zeros((DIM,), dtype=jnp.float32)}
    _L3_attn_in = _L3_attn_setup()

    def _L3_ffn_setup():
        import jax, jax.numpy as jnp
        import numpy as np
        B, S, D, F, E = (2, 256, 128, 512, 8)
        LN_EPS = 1e-05

        def _layer_norm(x, gamma, beta):
            mu = jnp.mean(x, axis=-1, keepdims=True)
            var = jnp.mean(jnp.square(x - mu), axis=-1, keepdims=True)
            return (x - mu) * jax.lax.rsqrt(var + LN_EPS) * gamma + beta
        key = jax.random.key(seed)
        ks = jax.random.split(key, 8)

        def xavier(k, shape):
            fan_in, fan_out = (shape[-1], shape[-2])
            a = jnp.sqrt(6.0 / (fan_in + fan_out))
            return jax.random.uniform(k, shape, jnp.float32, -a, a)
        return {'tgt': jax.random.normal(ks[0], (B, S, D), jnp.float32), 'Wr': xavier(ks[1], (E, D)), 'br': jnp.zeros((E,), jnp.float32), 'W1': xavier(ks[2], (E, F, D)), 'b1': jnp.zeros((E, F), jnp.float32), 'W2': xavier(ks[3], (E, D, F)), 'b2': jnp.zeros((E, D), jnp.float32), 'gamma': jnp.ones((D,), jnp.float32), 'beta': jnp.zeros((D,), jnp.float32)}
    _L3_ffn_in = _L3_ffn_setup()
    _d = {'L0_attn_x': _L0_attn_in['x'], 'L0_attn_w_qkv': _L0_attn_in['w_qkv'], 'L0_attn_b_qkv': _L0_attn_in['b_qkv'], 'L0_attn_w_out': _L0_attn_in['w_out'], 'L0_attn_b_out': _L0_attn_in['b_out'], 'L0_ffn_w1_w': _L0_ffn_in['w1_w'], 'L0_ffn_w1_s': _L0_ffn_in['w1_s'], 'L0_ffn_w2_w': _L0_ffn_in['w2_w'], 'L0_ffn_w2_s': _L0_ffn_in['w2_s'], 'L0_ffn_h1_w': _L0_ffn_in['h1_w'], 'L0_ffn_h1_s': _L0_ffn_in['h1_s'], 'L0_ffn_h2_w': _L0_ffn_in['h2_w'], 'L0_ffn_h2_s': _L0_ffn_in['h2_s'], 'L0_ffn_w3_w': _L0_ffn_in['w3_w'], 'L0_ffn_w3_s': _L0_ffn_in['w3_s'], 'L1_attn_in_proj_w': _L1_attn_in['in_proj_w'], 'L1_attn_conv_w': _L1_attn_in['conv_w'], 'L1_attn_conv_b': _L1_attn_in['conv_b'], 'L1_attn_x_proj_w': _L1_attn_in['x_proj_w'], 'L1_attn_dt_proj_w': _L1_attn_in['dt_proj_w'], 'L1_attn_dt_proj_b': _L1_attn_in['dt_proj_b'], 'L1_attn_out_proj_w': _L1_attn_in['out_proj_w'], 'L1_attn_A_log': _L1_attn_in['A_log'], 'L1_attn_D_param': _L1_attn_in['D_param'], 'L1_ffn_gate_w': _L1_ffn_in['gate_w'], 'L1_ffn_gate_b': _L1_ffn_in['gate_b'], 'L1_ffn_w1': _L1_ffn_in['w1'], 'L1_ffn_b1': _L1_ffn_in['b1'], 'L1_ffn_w2': _L1_ffn_in['w2'], 'L1_ffn_b2': _L1_ffn_in['b2'], 'L1_ffn_w3': _L1_ffn_in['w3'], 'L1_ffn_b3': _L1_ffn_in['b3'], 'L2_attn_in_proj_w': _L2_attn_in['in_proj_w'], 'L2_attn_conv_w': _L2_attn_in['conv_w'], 'L2_attn_conv_b': _L2_attn_in['conv_b'], 'L2_attn_x_proj_w': _L2_attn_in['x_proj_w'], 'L2_attn_dt_proj_w': _L2_attn_in['dt_proj_w'], 'L2_attn_dt_proj_b': _L2_attn_in['dt_proj_b'], 'L2_attn_A_log': _L2_attn_in['A_log'], 'L2_attn_Dp': _L2_attn_in['Dp'], 'L2_attn_out_proj_w': _L2_attn_in['out_proj_w'], 'L2_attn_mnorm_g': _L2_attn_in['mnorm_g'], 'L2_attn_mnorm_b': _L2_attn_in['mnorm_b'], 'L2_attn_n1_g': _L2_attn_in['n1_g'], 'L2_attn_n1_b': _L2_attn_in['n1_b'], 'L2_attn_n2_g': _L2_attn_in['n2_g'], 'L2_attn_n2_b': _L2_attn_in['n2_b'], 'L2_attn_n3_g': _L2_attn_in['n3_g'], 'L2_attn_n3_b': _L2_attn_in['n3_b'], 'L2_attn_ffn_w1': _L2_attn_in['ffn_w1'], 'L2_attn_ffn_w2': _L2_attn_in['ffn_w2'], 'L2_attn_fe_w': _L2_attn_in['fe_w'], 'L2_attn_fe_b': _L2_attn_in['fe_b'], 'L2_ffn_router_w': _L2_ffn_in['router_w'], 'L2_ffn_w1': _L2_ffn_in['w1'], 'L2_ffn_w2': _L2_ffn_in['w2'], 'L2_ffn_shared_gate_up': _L2_ffn_in['shared_gate_up'], 'L2_ffn_shared_down': _L2_ffn_in['shared_down'], 'L2_ffn_shared_gate_w': _L2_ffn_in['shared_gate_w'], 'L3_attn_Wq': _L3_attn_in['Wq'], 'L3_attn_Wk': _L3_attn_in['Wk'], 'L3_attn_Wv': _L3_attn_in['Wv'], 'L3_attn_Wp': _L3_attn_in['Wp'], 'L3_attn_bp': _L3_attn_in['bp'], 'L3_attn_conv_w': _L3_attn_in['conv_w'], 'L3_attn_conv_b': _L3_attn_in['conv_b'], 'L3_ffn_Wr': _L3_ffn_in['Wr'], 'L3_ffn_br': _L3_ffn_in['br'], 'L3_ffn_W1': _L3_ffn_in['W1'], 'L3_ffn_b1': _L3_ffn_in['b1'], 'L3_ffn_W2': _L3_ffn_in['W2'], 'L3_ffn_b2': _L3_ffn_in['b2'], 'L3_ffn_gamma': _L3_ffn_in['gamma'], 'L3_ffn_beta': _L3_ffn_in['beta']}
    _x0 = _d['L0_attn_x']
    _d['L0_attn_x'] = jax.random.normal(jax.random.fold_in(jax.random.key(seed), 1), (4, 1024, 128), dtype=_x0.dtype)
    del _x0
    return _d

def reference(L0_attn_x, L0_attn_w_qkv, L0_attn_b_qkv, L0_attn_w_out, L0_attn_b_out, L0_ffn_w1_w, L0_ffn_w1_s, L0_ffn_w2_w, L0_ffn_w2_s, L0_ffn_h1_w, L0_ffn_h1_s, L0_ffn_h2_w, L0_ffn_h2_s, L0_ffn_w3_w, L0_ffn_w3_s, L1_attn_in_proj_w, L1_attn_conv_w, L1_attn_conv_b, L1_attn_x_proj_w, L1_attn_dt_proj_w, L1_attn_dt_proj_b, L1_attn_out_proj_w, L1_attn_A_log, L1_attn_D_param, L1_ffn_gate_w, L1_ffn_gate_b, L1_ffn_w1, L1_ffn_b1, L1_ffn_w2, L1_ffn_b2, L1_ffn_w3, L1_ffn_b3, L2_attn_in_proj_w, L2_attn_conv_w, L2_attn_conv_b, L2_attn_x_proj_w, L2_attn_dt_proj_w, L2_attn_dt_proj_b, L2_attn_A_log, L2_attn_Dp, L2_attn_out_proj_w, L2_attn_mnorm_g, L2_attn_mnorm_b, L2_attn_n1_g, L2_attn_n1_b, L2_attn_n2_g, L2_attn_n2_b, L2_attn_n3_g, L2_attn_n3_b, L2_attn_ffn_w1, L2_attn_ffn_w2, L2_attn_fe_w, L2_attn_fe_b, L2_ffn_router_w, L2_ffn_w1, L2_ffn_w2, L2_ffn_shared_gate_up, L2_ffn_shared_down, L2_ffn_shared_gate_w, L3_attn_Wq, L3_attn_Wk, L3_attn_Wv, L3_attn_Wp, L3_attn_bp, L3_attn_conv_w, L3_attn_conv_b, L3_ffn_Wr, L3_ffn_br, L3_ffn_W1, L3_ffn_b1, L3_ffn_W2, L3_ffn_b2, L3_ffn_gamma, L3_ffn_beta):

    def _L0_attn_ref(x, w_qkv, b_qkv, w_out, b_out):
        import jax, jax.numpy as jnp
        import numpy as np
        THETA = 10000.0

        def _rope_tables(seq_len, head_dim):
            dims = jnp.arange(0, head_dim, 2, dtype=jnp.float32)
            inv_freq = 1.0 / THETA ** (dims / head_dim)
            angles = jnp.arange(seq_len, dtype=jnp.float32)[:, None] * inv_freq[None, :]
            return (jnp.cos(angles), jnp.sin(angles))

        def _apply_rope(x, cos, sin):
            B, H, S, hd = x.shape
            xp = x.reshape(B, H, S, hd // 2, 2)
            x0, x1 = (xp[..., 0], xp[..., 1])
            c = cos[None, None, :, :]
            s = sin[None, None, :, :]
            r0 = x0 * c - x1 * s
            r1 = x0 * s + x1 * c
            return jnp.stack([r0, r1], axis=-1).reshape(B, H, S, hd)
        B, S, D = x.shape
        n_heads = 16
        hd = D // n_heads
        qkv = x @ w_qkv.T + b_qkv
        q, k, v = jnp.split(qkv, 3, axis=-1)

        def to_heads(t):
            return t.reshape(B, S, n_heads, hd).transpose(0, 2, 1, 3)
        q, k, v = (to_heads(q), to_heads(k), to_heads(v))
        cos, sin = _rope_tables(S, hd)
        q = _apply_rope(q, cos, sin)
        k = _apply_rope(k, cos, sin)
        scores = jnp.einsum('bhsd,bhtd->bhst', q, k) / jnp.sqrt(jnp.float32(hd))
        causal = jnp.tril(jnp.ones((S, S), dtype=bool))
        scores = jnp.where(causal[None, None, :, :], scores, -jnp.inf)
        attn = jax.nn.softmax(scores, axis=-1)
        out = jnp.einsum('bhst,bhtd->bhsd', attn, v)
        out = out.transpose(0, 2, 1, 3).reshape(B, S, D)
        return out @ w_out.T + b_out

    def _L0_ffn_ref(x, w1_w, w1_s, w2_w, w2_s, h1_w, h1_s, h2_w, h2_s, w3_w, w3_s):
        import jax, jax.numpy as jnp
        import numpy as np
        D_IN, D_HID = (128, 512)

        def _ternary(key, shape):
            return jax.random.randint(key, shape, -1, 2).astype(jnp.float32)

        def _tlin(x, w, s):
            return jnp.einsum('bsi,oi->bso', x, w) * s
        h = jax.nn.silu(_tlin(x, w1_w, w1_s)) * _tlin(x, w2_w, w2_s)
        h = jax.nn.gelu(_tlin(h, h1_w, h1_s), approximate=False)
        h = jax.nn.gelu(_tlin(h, h2_w, h2_s), approximate=False)
        return _tlin(h, w3_w, w3_s)

    def _L1_attn_ref(x, in_proj_w, conv_w, conv_b, x_proj_w, dt_proj_w, dt_proj_b, out_proj_w, A_log, D_param):
        import jax, jax.numpy as jnp
        import numpy as np
        from jax import lax
        B, L, _ = x.shape
        d_inner = D_param.shape[0]
        d_conv = conv_w.shape[-1]
        xz = x @ in_proj_w.T
        x_p, z = jnp.split(xz, 2, axis=-1)
        xc = jnp.transpose(x_p, (0, 2, 1))
        xc = lax.conv_general_dilated(xc, conv_w, window_strides=(1,), padding=[(d_conv - 1, 0)], dimension_numbers=('NCH', 'OIH', 'NCH'), feature_group_count=d_inner)
        xc = xc + conv_b[None, :, None]
        xc = jax.nn.silu(jnp.transpose(xc, (0, 2, 1)))
        dt = jax.nn.softplus(xc @ dt_proj_w.T + dt_proj_b)
        BC = xc @ x_proj_w.T
        B_ssm, C_ssm = jnp.split(BC, 2, axis=-1)
        s = jnp.sum(xc * dt, axis=-1, keepdims=True)
        y = s * B_ssm
        y = y * C_ssm
        y = jnp.sum(y, axis=-1, keepdims=True) + xc * D_param
        y = y * jax.nn.silu(z)
        return y @ out_proj_w.T

    def _L1_ffn_ref(x, gate_w, gate_b, w1, b1, w2, b2, w3, b3):
        import jax, jax.numpy as jnp
        import numpy as np
        B, S, D, O, E, K = (2, 256, 128, 128, 8, 2)
        probs = jax.nn.softmax(x @ gate_w.T + gate_b, axis=-1)
        _, topi = jax.lax.top_k(probs, K)
        onehot = jax.nn.one_hot(topi, E, dtype=probs.dtype)
        cw = jnp.einsum('bske,bsk->bse', onehot, probs[..., :K])
        out = jnp.zeros(x.shape[:2] + (O,), x.dtype)
        for e in range(E):
            h = jax.nn.relu(x @ w1[e] + b1[e])
            h = jax.nn.relu(h @ w2[e] + b2[e])
            h = h @ w3[e] + b3[e]
            out = out + cw[..., e:e + 1] * h
        return out

    def _L2_attn_ref(src, in_proj_w, conv_w, conv_b, x_proj_w, dt_proj_w, dt_proj_b, A_log, Dp, out_proj_w, mnorm_g, mnorm_b, n1_g, n1_b, n2_g, n2_b, n3_g, n3_b, ffn_w1, ffn_w2, fe_w, fe_b):
        import jax, jax.numpy as jnp
        import numpy as np
        from jax import lax
        D_MODEL = 128
        D_IN = 128
        N_STATE = 16
        DT_RANK = 64
        D_FFN = 512
        BATCH, SEQ = (2, 256)

        def _ln(x, g, b, eps=1e-05):
            m = x.mean(-1, keepdims=True)
            v = ((x - m) ** 2).mean(-1, keepdims=True)
            return (x - m) / jnp.sqrt(v + eps) * g + b

        def _mamba(x, in_proj_w, conv_w, conv_b, x_proj_w, dt_proj_w, dt_proj_b, A_log, Dp, out_proj_w):
            B, L, _ = x.shape
            xz = x @ in_proj_w.T
            x_in, z = jnp.split(xz, 2, axis=-1)
            x_prev = jnp.pad(x_in, ((0, 0), (1, 0), (0, 0)))[:, :L]
            x_c = jax.nn.silu(x_prev * conv_w[:, 0] + x_in * conv_w[:, 1] + conv_b)
            x_dbl = x_c @ x_proj_w.T
            dt, Bm, Cm = jnp.split(x_dbl, [DT_RANK, DT_RANK + N_STATE], axis=-1)
            delta = jax.nn.softplus(dt @ dt_proj_w.T + dt_proj_b)
            A = -jnp.exp(A_log)
            deltaA = jnp.exp(delta[..., None] * A)
            dBu = delta[..., None] * Bm[:, :, None, :] * x_c[..., None]

            def step(h, t):
                dA_t, dBu_t, C_t = t
                h = dA_t * h + dBu_t
                y = jnp.einsum('bdn,bn->bd', h, C_t)
                return (h, y)
            h0 = jnp.zeros((B, D_IN, N_STATE), x.dtype)
            _, ys = lax.scan(step, h0, (deltaA.transpose(1, 0, 2, 3), dBu.transpose(1, 0, 2, 3), Cm.transpose(1, 0, 2)))
            y = ys.transpose(1, 0, 2)
            y = (y + x_c * Dp) * jax.nn.silu(z)
            return y @ out_proj_w.T
        h = _mamba(_ln(src, n1_g, n1_b), in_proj_w, conv_w, conv_b, x_proj_w, dt_proj_w, dt_proj_b, A_log, Dp, out_proj_w)
        src = src + _ln(h, mnorm_g, mnorm_b)
        f = _ln(src, n2_g, n2_b) @ ffn_w1.T
        f = jnp.where(f >= 0, f, 0.01 * f) @ ffn_w2.T
        src = src + f
        src = src + (_ln(src, n3_g, n3_b) @ fe_w.T + fe_b)
        return src

    def _L2_ffn_ref(x, router_w, w1, w2, shared_gate_up, shared_down, shared_gate_w):
        import jax, jax.numpy as jnp
        import numpy as np
        D = 128
        F = 128
        E = 8
        K = 2
        B, T = (2, 256)

        def _moe_forward(x, router_w, w1, w2, shared_gate_up, shared_down, shared_gate_w):
            b, t, d = x.shape
            xf = x.reshape(-1, d)
            n = xf.shape[0]
            logits = xf @ router_w
            probs = jax.nn.softmax(logits, axis=-1)
            topw, topi = jax.lax.top_k(probs, K)
            combine = jnp.zeros((n, E), dtype=probs.dtype).at[jnp.arange(n)[:, None], topi].add(topw)
            h = jax.nn.silu(jnp.einsum('nd,edf->nef', xf, w1))
            ye = jnp.einsum('nef,efd->ned', h, w2)
            routed = jnp.einsum('ne,ned->nd', combine, ye)
            gu = xf @ shared_gate_up
            gate, up = (gu[:, :F], gu[:, F:])
            shared = jax.nn.silu(gate) * up @ shared_down
            shared = jax.nn.sigmoid(xf @ shared_gate_w) * shared
            return (routed + shared).reshape(b, t, d)
        return _moe_forward(x, router_w, w1, w2, shared_gate_up, shared_down, shared_gate_w)

    def _L3_attn_ref(x, Wq, Wk, Wv, Wp, bp, conv_w, conv_b):
        import jax, jax.numpy as jnp
        import numpy as np
        DIM = 128
        HEADS = 16
        HEAD_DIM = DIM // HEADS
        B, S = (4, 512)
        b, s, d = x.shape

        def split_heads(t):
            return t.reshape(b, s, HEADS, HEAD_DIM).transpose(0, 2, 1, 3)
        q = split_heads(x @ Wq.T)
        k = split_heads(x @ Wk.T)
        v = split_heads(x @ Wv.T)
        q = jax.nn.elu(q) + 1.0
        k = jax.nn.elu(k) + 1.0
        kv_state = jnp.einsum('bhnd,bhne->bhde', k, v)
        k_state = k.sum(axis=2)
        attn_out = jnp.einsum('bhnd,bhde->bhne', q, kv_state)
        denom = jnp.maximum(jnp.einsum('bhnd,bhd->bhn', q, k_state), 1e-06)[..., None]
        attn_out = (attn_out / denom).transpose(0, 2, 1, 3).reshape(b, s, d)
        xp = jnp.pad(x, ((0, 0), (1, 1), (0, 0)))
        local = xp[:, :-2, :] * conv_w[:, 0] + xp[:, 1:-1, :] * conv_w[:, 1] + xp[:, 2:, :] * conv_w[:, 2] + conv_b
        return (attn_out + local) @ Wp.T + bp

    def _L3_ffn_ref(tgt, Wr, br, W1, b1, W2, b2, gamma, beta):
        import jax, jax.numpy as jnp
        import numpy as np
        B, S, D, F, E = (2, 256, 128, 512, 8)
        LN_EPS = 1e-05

        def _layer_norm(x, gamma, beta):
            mu = jnp.mean(x, axis=-1, keepdims=True)
            var = jnp.mean(jnp.square(x - mu), axis=-1, keepdims=True)
            return (x - mu) * jax.lax.rsqrt(var + LN_EPS) * gamma + beta
        logits = jnp.einsum('bsd,ed->bse', tgt, Wr) + br
        top_v, top_i = jax.lax.top_k(logits, 2)
        top_w = jax.nn.softmax(top_v, axis=-1)
        n_exp = logits.shape[-1]
        router_w = jnp.sum(jax.nn.one_hot(top_i, n_exp, dtype=top_w.dtype) * top_w[..., None], axis=-2)
        h = jnp.einsum('bsd,efd->bsef', tgt, W1) + b1
        h = jax.nn.relu(h)
        o = jnp.einsum('bsef,edf->bsed', h, W2) + b2
        tgt2 = jnp.einsum('bsed,bse->bsd', o, router_w)
        return _layer_norm(tgt + tgt2, gamma, beta)
    x = L0_attn_x
    x = x + 0.5 * _L0_ffn_ref(_layernorm(x, axis=-1), L0_ffn_w1_w, L0_ffn_w1_s, L0_ffn_w2_w, L0_ffn_w2_s, L0_ffn_h1_w, L0_ffn_h1_s, L0_ffn_h2_w, L0_ffn_h2_s, L0_ffn_w3_w, L0_ffn_w3_s)
    x = x + _L0_attn_ref(_layernorm(x, axis=-1), L0_attn_w_qkv, L0_attn_b_qkv, L0_attn_w_out, L0_attn_b_out)
    x = x + 0.5 * _L0_ffn_ref(_layernorm(x, axis=-1), L0_ffn_w1_w, L0_ffn_w1_s, L0_ffn_w2_w, L0_ffn_w2_s, L0_ffn_h1_w, L0_ffn_h1_s, L0_ffn_h2_w, L0_ffn_h2_s, L0_ffn_w3_w, L0_ffn_w3_s)
    x = x + 0.5 * _L1_ffn_ref(_layernorm(x, axis=-1), L1_ffn_gate_w, L1_ffn_gate_b, L1_ffn_w1, L1_ffn_b1, L1_ffn_w2, L1_ffn_b2, L1_ffn_w3, L1_ffn_b3)
    x = x + _L1_attn_ref(_layernorm(x, axis=-1), L1_attn_in_proj_w, L1_attn_conv_w, L1_attn_conv_b, L1_attn_x_proj_w, L1_attn_dt_proj_w, L1_attn_dt_proj_b, L1_attn_out_proj_w, L1_attn_A_log, L1_attn_D_param)
    x = x + 0.5 * _L1_ffn_ref(_layernorm(x, axis=-1), L1_ffn_gate_w, L1_ffn_gate_b, L1_ffn_w1, L1_ffn_b1, L1_ffn_w2, L1_ffn_b2, L1_ffn_w3, L1_ffn_b3)
    x = x + 0.5 * _L2_ffn_ref(_layernorm(x, axis=-1), L2_ffn_router_w, L2_ffn_w1, L2_ffn_w2, L2_ffn_shared_gate_up, L2_ffn_shared_down, L2_ffn_shared_gate_w)
    x = x + _L2_attn_ref(_layernorm(x, axis=-1), L2_attn_in_proj_w, L2_attn_conv_w, L2_attn_conv_b, L2_attn_x_proj_w, L2_attn_dt_proj_w, L2_attn_dt_proj_b, L2_attn_A_log, L2_attn_Dp, L2_attn_out_proj_w, L2_attn_mnorm_g, L2_attn_mnorm_b, L2_attn_n1_g, L2_attn_n1_b, L2_attn_n2_g, L2_attn_n2_b, L2_attn_n3_g, L2_attn_n3_b, L2_attn_ffn_w1, L2_attn_ffn_w2, L2_attn_fe_w, L2_attn_fe_b)
    x = x + 0.5 * _L2_ffn_ref(_layernorm(x, axis=-1), L2_ffn_router_w, L2_ffn_w1, L2_ffn_w2, L2_ffn_shared_gate_up, L2_ffn_shared_down, L2_ffn_shared_gate_w)
    x = x + 0.5 * _L3_ffn_ref(_layernorm(x, axis=-1), L3_ffn_Wr, L3_ffn_br, L3_ffn_W1, L3_ffn_b1, L3_ffn_W2, L3_ffn_b2, L3_ffn_gamma, L3_ffn_beta)
    x = x + _L3_attn_ref(_layernorm(x, axis=-1), L3_attn_Wq, L3_attn_Wk, L3_attn_Wv, L3_attn_Wp, L3_attn_bp, L3_attn_conv_w, L3_attn_conv_b)
    x = x + 0.5 * _L3_ffn_ref(_layernorm(x, axis=-1), L3_ffn_Wr, L3_ffn_br, L3_ffn_W1, L3_ffn_b1, L3_ffn_W2, L3_ffn_b2, L3_ffn_gamma, L3_ffn_beta)
    return x

_drawn_inputs = setup_inputs


def setup_inputs(seed=0):
    import zlib

    import numpy as np

    out = dict(_drawn_inputs(seed))
    spreads = {'L1_attn_D_param': (1.0, 0.2),
     'L1_ffn_gate_b': (0.0, 0.1),
     'L1_ffn_b1': (0.0, 0.1),
     'L1_ffn_b2': (0.0, 0.1),
     'L1_ffn_b3': (0.0, 0.1),
     'L2_attn_conv_b': (0.0, 0.1),
     'L2_attn_Dp': (1.0, 0.2),
     'L2_attn_mnorm_g': (1.0, 0.2),
     'L2_attn_mnorm_b': (0.0, 0.1),
     'L2_attn_n1_g': (1.0, 0.2),
     'L2_attn_n1_b': (0.0, 0.1),
     'L2_attn_n2_g': (1.0, 0.2),
     'L2_attn_n2_b': (0.0, 0.1),
     'L2_attn_n3_g': (1.0, 0.2),
     'L2_attn_n3_b': (0.0, 0.1),
     'L2_attn_fe_b': (0.0, 0.1),
     'L3_attn_bp': (0.0, 0.1),
     'L3_attn_conv_b': (0.0, 0.1),
     'L3_ffn_br': (0.0, 0.1),
     'L3_ffn_b1': (0.0, 0.1),
     'L3_ffn_b2': (0.0, 0.1),
     'L3_ffn_gamma': (1.0, 0.2),
     'L3_ffn_beta': (0.0, 0.1)}
    factors = {}
    for name, (base, spread) in spreads.items():
        noise = np.random.default_rng([zlib.crc32(name.encode()), seed]).standard_normal(out[name].shape)
        drawn = base * np.exp(spread * noise) if base else spread * noise
        out[name] = jnp.asarray(drawn.astype(out[name].dtype))
    for name, factor in factors.items():
        out[name] = (out[name] * factor).astype(out[name].dtype)
    return out
```

```python
import concourse.bass as bass
from concourse import mybir

P = 128
T = 4096
NB, S = 4, 1024
C = 512
NC_ = T // C
TILE = 128
TPC = C // TILE
NH, HD = 16, 8
E8 = 8
NEG = -1e30
EPS = 1e-5
EULER = 2.718281828459045

F32, F32R, BF16 = mybir.dt.float32, mybir.dt.float32r, mybir.dt.bfloat16
ALU = mybir.AluOpType
ACT = mybir.ActivationFunctionType
AX = mybir.AxisListType

L0W = {"w1": 0, "w2": 512, "h1": 1024, "h2": 1024 + 2048, "w3": 1024 + 4096}
L0W_COLS = 1024 + 4096 + 512
L1W_COLS = E8 * 3 * P
L2W_GU, L2W_DOWN = E8 * 2 * P, E8 * 2 * P + 2 * P
L2W_COLS = L2W_DOWN + P
L3W_COLS = 8 * P
N0 = {"q": 0, "qs": 128, "k": 256, "ks": 384, "v": 512, "o": 640}
N0_COLS = 768
N1 = {"in": 0, "dt": 512, "x": 1024, "o": 1088}
N1_COLS = 1344
N2 = {"in": 0, "xdt": 256, "xbc": 320, "dt": 416, "o": 544, "f1": 672, "f2": 1184, "fe": 1696}
N2_COLS = 1824
N3 = {"q": 0, "k": 128, "v": 256, "p": 384}
N3_COLS = 512

_at = 0
COLS = {}
for _name, _n in [("s1", 4), ("s2", 4), ("h1s", 4), ("h2s", 4), ("w3s", 1),
                  ("bq", 1), ("bqs", 1), ("bk", 1), ("bks", 1), ("bo", 1),
                  ("l1b1", 8), ("l1b2", 8), ("l1b3", 8),
                  ("m1conv", 8), ("m1cb", 2), ("m1dtb", 2), ("m1D", 2),
                  ("m2conv", 2), ("m2cb", 1), ("m2dtb", 1), ("m2D", 1), ("m2A", 16),
                  ("mg", 1), ("mb", 1), ("n1g", 1), ("n1b", 1), ("n2g", 1), ("n2b", 1), ("n3g", 1), ("n3b", 1),
                  ("feb", 1), ("c3w", 3), ("c3b", 1), ("bp", 1),
                  ("l3b1", 32), ("l3b2", 8), ("l3g", 1), ("l3be", 1)]:
    COLS[_name] = _at
    _at += _n
NCOLS = _at
ROWS = {"br1": 0, "br3": 8, "code": 16, "bv": 24}
NROWS = 24 + P
MATS = {"ident": 0, "heads": 128, "num": 256, "den": 480, "centre": 704, "mask_st": 832, "mask_ts": 960, "pick": 1088}
KEPT_MATS = 704
NMATS = 1088 + 32
RW = {"l1": 0, "l2": 8, "l3": 17}
NRW = 25

LAST = 12


class Token:

    def __init__(self, sem, value):
        self.sem, self.value = sem, value


class Queue:

    def __init__(self, sem):
        self.sem, self.count, self.items, self.waited = sem, 0, [], {}

    def do(self, make, after=(), signal=True):
        waits = []
        for t in after:
            if t is not None and self.waited.get(id(t.sem), 0) < t.value:
                self.waited[id(t.sem)] = t.value
                waits = [w for w in waits if w.sem is not t.sem] + [t]
        if signal:
            self.count += 1
        self.items.append((waits, make, signal))
        return Token(self.sem, self.count) if signal else None

    def mark(self):
        return Token(self.sem, self.count)

    def replay(self, eng):
        for waits, make, signal in self.items:
            for t in waits:
                eng.wait_ge(t.sem, t.value)
            ins = make(eng)
            if signal:
                ins.then_inc(self.sem, 1)


class DmaQueue:

    def __init__(self, sems):
        self.sems, self.n, self.items, self.waited = sems, 0, [], {}

    def do(self, out, in_, after=()):
        waits = []
        for t in after:
            if t is not None and self.waited.get(id(t.sem), 0) < t.value:
                self.waited[id(t.sem)] = t.value
                waits = [w for w in waits if w.sem is not t.sem] + [t]
        sem = self.sems[self.n % len(self.sems)]
        turn = self.n // len(self.sems)
        if turn and self.waited.get(id(sem), 0) < 16 * turn:
            waits.append(Token(sem, 16 * turn))
            self.waited[id(sem)] = 16 * turn
        self.items.append((waits, out, in_, sem))
        self.n += 1
        return Token(sem, 16 * (turn + 1))

    def replay(self, eng):
        for waits, out, in_, sem in self.items:
            for t in waits:
                eng.wait_ge(t.sem, t.value)
            eng.dma_start(out, in_).then_inc(sem, 16)


class Slots:

    def __init__(self, items):
        self.free = [(x, ()) for x in items]

    def take(self, n=1):
        while len(self.free) < n:
            yield
        got = [self.free.pop(0) for _ in range(n)]
        return got[0] if n == 1 else got

    def give(self, item, readers):
        self.free.append((item, tuple(readers)))


class Banks:

    def __init__(self, psum):
        self.psum = psum
        self.free = [(i, ()) for i in range(8)]

    def take(self):
        while not self.free:
            yield
        i, readers = self.free.pop(0)
        return i, readers

    def take_pair(self):
        while True:
            held = dict(self.free)
            for i, _ in self.free:
                j = i ^ 1
                if j in held:
                    a = min(i, j)
                    readers = tuple(held[i]) + tuple(held[j])
                    self.free = [x for x in self.free if x[0] not in (i, j)]
                    return a, readers
            yield

    def give(self, i, readers):
        self.free.append((i, tuple(readers)))

    def give_pair(self, i, readers):
        self.give(i, readers)
        self.give(i + 1, readers)


class Gate:

    def __init__(self, n):
        self.n = n

    def enter(self):
        while not self.n:
            yield
        self.n -= 1

    def leave(self):
        self.n += 1


def run_jobs(jobs, width):
    done, active, waiting = set(), [], list(jobs)
    idle = 0
    while waiting or active:
        while waiting and len(active) < width and all(d in done for d in waiting[0][2]):
            name, make, _ = waiting.pop(0)
            active.append((name, make()))
        before = (len(waiting), len(active))
        moved = False
        for job in list(active):
            try:
                if next(job[1]) is not None:
                    moved = True
            except StopIteration:
                active.remove(job)
                done.add(job[0])
                moved = True
        idle = 0 if moved or before != (len(waiting), len(active)) else idle + 1
        assert idle < 5, ("no job can go on", [a[0] for a in active])


GO = 1



def build(nc, x_t, w0, w1, w2, w3, n0, n1, n2, n3, rw, cols, rows, mats, rope, zero, out):
    place = [nc.sbuf_base + 63 & ~63]

    def at(name, shape, dt, offset=None):
        size = 2 if dt == BF16 else 4
        for n in shape[1:]:
            size *= n
        where = place[0] if offset is None else offset
        if offset is None:
            place[0] = where + (size + 63 & ~63)
        return nc.alloc_sbuf_tensor_at(name, shape, dt, offset=where)

    X = at("x_res", [P, T], F32)
    colv = at("feature_cols", [P, NCOLS], F32)
    rowv = at("row_consts", [P, NROWS], F32)
    matf = at("const_mats", [P, KEPT_MATS], F32)
    matr = at("const_mats_r", [P, 2 * P], F32R)
    matb = at("const_mats_bf", [P, 3 * P], BF16)
    pickb = at("pick_bf", [96, 32], BF16)
    routerw = at("router_w", [P, NRW], F32)
    inv_width = at("inv_width", [P, 1], F32)
    minus_half = at("minus_half", [P, TPC], F32)
    euler = at("euler", [P, TPC * 9], F32)
    neg_a = at("neg_exp_alog", [P, 16], F32)
    s3half = at("half_w3s", [P, 1], F32)
    work = at("work_tiles", [P, 18, C], F32)
    pairs_t = at("pair_tiles", [P, 13, 2, C], F32R)
    small = at("small_tiles", [P, 6, 8], F32)
    smallr = at("small_tiles_r", [P, 6, 8], F32R)
    NS = 16
    w0n = at("attn0_weights", [P, N0_COLS], F32)
    region = place[0]
    w0r = at("ffn0_weights", [P, 2, L0W_COLS], F32R, region)
    attn_at = region + 8 * L0W_COLS
    NSTACK = 3
    qs_t = at("q_stacks", [P, NSTACK, 2, S], BF16, attn_at)
    ks_t = at("k_stacks", [P, NSTACK, 4, S], BF16, attn_at + 4 * NSTACK * S)
    v_at = attn_at + 12 * NSTACK * S
    v_t = at("v_rows", [P, 8, 176], F32, v_at)
    rope_t = at("rope", [P, 2, S], F32, v_at + 8 * 176 * 4)
    end_a = v_at + 8 * 176 * 4 + 8 * S
    w1r = at("moe1_weights", [P, 2, L1W_COLS], F32R, attn_at)
    w2r = at("moe2_weights", [P, 2, L2W_COLS], F32R, attn_at + 8 * L1W_COLS)
    w1n = at("mamba1_weights", [P, N1_COLS], F32, region)
    w2n = at("mamba2_weights", [P, N2_COLS], F32, region + 4 * N1_COLS)
    w3n = at("attn3_weights", [P, N3_COLS], F32, region + 4 * (N1_COLS + N2_COLS))
    free_b = region + 4 * (N1_COLS + N2_COLS + N3_COLS)
    EXTRA = 12
    extra = at("more_work_tiles", [P, EXTRA, C], F32, free_b)
    odds = free_b + EXTRA * 4 * C
    ones = at("ones", [P, P], F32, odds)
    tails = at("conv_tails", [P, NC_, 2, 4], F32, odds + 4 * P)
    states = at("scan_states", [P, NB, NS], F32, odds + 4 * P + 32 * NC_)
    NEXP = 3
    w3r = at("moe3_weights", [P, NEXP, 2, L3W_COLS], F32R, free_b)
    assert max(end_a, free_b + EXTRA * 4 * C, attn_at + 8 * (L1W_COLS + L2W_COLS)) <= 229344, end_a
    assert odds + 4 * P + 32 * NC_ + 4 * NB * NS <= attn_at and NEXP * 8 * L3W_COLS <= EXTRA * 4 * C
    psum = nc.alloc_psum_tensor("banks", [P, 8, C], F32)

    gates_d = nc.dram_tensor("gates_d", [6 * NC_, 9 * C], F32, kind="Internal").ap()
    parts_d = nc.dram_tensor("parts_d", [NB, 2, 3, P, S], BF16, kind="Internal").ap()
    shift_d = nc.dram_tensor("shift_d", [NB, NH, 8, TILE], BF16, kind="Internal").ap()

    pe = Queue(nc.alloc_semaphore("pe_done"))
    act = Queue(nc.alloc_semaphore("act_done"))
    dve = Queue(nc.alloc_semaphore("dve_done"))
    pool = Queue(nc.alloc_semaphore("pool_done"))
    dma = DmaQueue([nc.alloc_semaphore(f"dma_done{i}") for i in range(32)])

    tiles = Slots([work[:, i, :] for i in range(12)])
    twins = Slots([work[:, i:i + 2, :] for i in range(12, 18, 2)])
    pairs = Slots([pairs_t[:, i, :, :] for i in range(13)])
    smalls = Slots(list(range(6)))
    banks = Banks(psum)

    def col(name, i=0):
        return colv[:, COLS[name] + i:COLS[name] + i + 1]

    ident = matf[:, 0:P]
    heads = matf[:, MATS["heads"]:MATS["heads"] + P]
    ident_r, centre_r = matr[:, 0:P], matr[:, P:2 * P]
    ident_b, mask_st, mask_ts = matb[:, 0:P], matb[:, P:2 * P], matb[:, 2 * P:3 * P]

    def copy_act(o, i, after):
        return act.do(lambda e: e.activation(o, i, ACT.Copy), after)

    def func(f, o, i, after, **kw):
        return act.do(lambda e: e.activation(o, i, f, **kw), after)

    def copy_dve(o, i, after):
        return dve.do(lambda e: e.tensor_copy(o, i), after)

    def tt(o, a, b, op, after, q=None):
        return (q or dve).do(lambda e: e.tensor_tensor(o, a, b, op), after)

    def ts(o, a, s1, op0, after, s2=None, op1=None):
        if op1 is None:
            return dve.do(lambda e: e.tensor_scalar(o, a, s1, None, op0), after)
        return dve.do(lambda e: e.tensor_scalar(o, a, s1, s2, op0, op1), after)

    def stt(o, a, s, b, op0, op1, after):
        return dve.do(lambda e: e.scalar_tensor_tensor(out=o, in0=a, scalar=s, in1=b, op0=op0, op1=op1), after)

    def mm(o, l, r, start, stop, after=(), signal=False):
        return pe.do(lambda e: e.matmul(o, l, r, start=start, stop=stop), after, signal)

    def split(src, pair, after, free):
        hi = copy_act(pair[:, 0, :], src, [*after, *free])
        lo = tt(pair[:, 1, :], src, pair[:, 0, :].bitcast(F32), ALU.subtract, [hi, *after])
        return [hi, lo]

    def split_mm(o, terms, after):
        n = len(terms)
        for i, (wh, wl, pair, marks) in enumerate(terms):
            mm(o, wh, pair[:, 0, :], i == 0, False, [*after, marks[0]])
            mm(o, wl, pair[:, 0, :], False, False)
            done = mm(o, wh, pair[:, 1, :], False, i == n - 1, [marks[1]], i == n - 1)
        return done

    def full_mm(o, terms, after):
        n = len(terms)
        for i, (w, x, marks) in enumerate(terms):
            done = mm(o, w, x, i == 0, i == n - 1, [*after, *marks], i == n - 1)
        return done

    stage, sfree = None, ()
    d_cols = dma.do(colv[:, :], cols)
    d_rows = dma.do(rowv[:, :], rows)
    d_mats = dma.do(matf[:, :], mats[:, 0:KEPT_MATS])
    raw = work[:, 0, :]
    d_raw = dma.do(raw[:, 0:NMATS - KEPT_MATS], mats[:, KEPT_MATS:NMATS])
    d_rw = dma.do(routerw[:, :], rw)
    x_ready = [[dma.do(X[:, c * C:(c + 1) * C], x_t[:, c * C:(c + 1) * C])] for c in range(NC_)]
    c_ready = [copy_dve(ident_r, ident, [d_mats]), copy_dve(centre_r, raw[:, 0:P], [d_raw]),
               copy_dve(ident_b, ident, [d_mats]), copy_dve(matb[:, P:3 * P], raw[:, P:3 * P], [d_raw])]
    c_ready.append(copy_dve(pickb[:, :], raw[0:96, 3 * P:3 * P + 32], [d_raw]))
    for tile, value in ((inv_width, 1.0 / P), (minus_half, -0.5), (euler, EULER)):
        c_ready.append(dve.do(lambda e, tile=tile, value=value: e.memset(tile[:, :], value)))
    c_ready.append(ts(s3half[:, :], col("w3s"), 0.5, ALU.mult, [d_cols]))
    ready = [c_ready[-1], d_cols, d_rows, d_mats, d_rw]
    for q in (pe, act, dve, pool):
        q.first = ready
    tiles.free[0] = (tiles.free[0][0], (c_ready[-1],))

    def need(q):
        marks, q.first = q.first, ()
        return list(marks)

    def load_native(dst, src, after):
        return dma.do(dst[:, :], src, after)

    def load_split(dst, src, ncols, after, marks):
        for c0 in range(0, ncols, C):
            n = min(C, ncols - c0)
            t, tf = yield from tiles.take()
            d = dma.do(t[:, 0:n], src[:, c0:c0 + n], [*tf, *after])
            hi = copy_dve(dst[:, 0, c0:c0 + n], t[:, 0:n], [d, *after])
            lo = tt(dst[:, 1, c0:c0 + n], t[:, 0:n], dst[:, 0, c0:c0 + n].bitcast(F32), ALU.subtract, [hi])
            tiles.give(t, [hi, lo])
            marks.append(lo)
            yield GO

    def layernorm(src, after, gain=None, bias=None):
        pair, pf = yield from pairs.take()
        xs = split(src, pair, [*after, *need(act), *need(dve)], pf)
        b, bf = yield from banks.take()
        pc = psum[:, b, :]
        mm(pc, centre_r, pair[:, 0, :], True, False, [xs[0], *bf, *need(pe)])
        centred = mm(pc, centre_r, pair[:, 1, :], False, True, [xs[1]], True)
        pairs.give(pair, [centred])
        yield GO
        (sq, f1), (xc, f2) = yield from tiles.take(2)
        squared = func(ACT.Square, sq, pc, [centred, *f1])
        copied = copy_act(xc, pc, [centred, *f2])
        banks.give(b, [copied])
        yield GO
        b, bf = yield from banks.take()
        for t in range(TPC):
            var = mm(psum[:, b, t:t + 1], sq[:, t * TILE:(t + 1) * TILE], inv_width[:, :], True, True,
                     [squared, *bf], t == TPC - 1)
        tiles.give(sq, [var])
        k, kf = yield from smalls.take()
        s, r = small[:, k, :], smallr[:, k, :]
        veps = ts(s[:, 0:4], psum[:, b, 0:4], EPS, ALU.add, [var, *kf])
        rstd = tt(s[:, 4:8], s[:, 0:4], minus_half[:, :], ALU.pow, [veps, *need(pool)], pool)
        rhi = copy_dve(r[:, 0:4], s[:, 4:8], [rstd])
        rlo = tt(r[:, 4:8], s[:, 4:8], r[:, 0:4].bitcast(F32), ALU.subtract, [rhi])
        yield GO
        for t in range(TPC):
            for part in (0, 4):
                spread = mm(psum[:, b, t * TILE:(t + 1) * TILE], r[:, part + t:part + t + 1].broadcast_to([P, P]),
                            ident_r, part == 0, part == 4, [rlo], t == TPC - 1 and part == 4)
        smalls.give(k, [spread])
        done = tt(xc, psum[:, b, :], xc, ALU.mult, [spread, copied])
        banks.give(b, [done])
        if gain is not None:
            done = ts(xc, xc, gain, ALU.mult, [done], bias, ALU.add)
        yield GO
        return xc, [done]

    w0_marks = []
    gate0 = Gate(2)

    def w0_parts(name, i):
        c0 = L0W[name] + i * P
        return w0r[:, 0, c0:c0 + P], w0r[:, 1, c0:c0 + P]

    def ffn0(c):
        xs = X[:, c * C:(c + 1) * C]
        xn, xm = yield from layernorm(xs, x_ready[c])
        yield from gate0.enter()
        xp, pf = yield from pairs.take()
        marks = split(xn, xp, xm, pf)
        tiles.give(xn, marks)
        while len(w0_marks) < L0W_COLS // C:
            yield
        hid = []
        for f in range(4):
            (b1, f1), (b2, f2) = (yield from banks.take()), (yield from banks.take())
            up = split_mm(psum[:, b1, :], [(*w0_parts("w1", f), xp, marks)], [*f1, w0_marks[0]])
            gt = split_mm(psum[:, b2, :], [(*w0_parts("w2", f), xp, marks)], [*f2, w0_marks[1]])
            h, hf = yield from tiles.take()
            a = func(ACT.Silu, h, psum[:, b1, :], [up, *hf], scale=col("s1", f))
            banks.give(b1, [a])
            g = stt(h, psum[:, b2, :], col("s2", f), h, ALU.mult, ALU.mult, [gt, a])
            banks.give(b2, [g])
            p, pf = yield from pairs.take()
            m = split(h, p, [g], pf)
            tiles.give(h, m)
            hid.append((p, m))
        pairs.give(xp, [gt])
        yield GO
        for name, scale in (("h1", "h1s"), ("h2", "h2s")):
            while len(pairs.free) < 4:
                yield
            nxt = []
            for o in range(4):
                b, bf = yield from banks.take()
                z = split_mm(psum[:, b, :], [(*w0_parts(name, 4 * k + o), *hid[k]) for k in range(4)],
                             [*bf, w0_marks[(L0W[name] + 2047) // C]])
                h, hf = yield from tiles.take()
                a = func(ACT.Gelu, h, psum[:, b, :], [z, *hf], scale=col(scale, o))
                banks.give(b, [a])
                p, pf = yield from pairs.take()
                m = split(h, p, [a], pf)
                tiles.give(h, m)
                nxt.append((p, m))
            for p, _ in hid:
                pairs.give(p, [z])
            hid = nxt
            yield GO
        b, bf = yield from banks.take()
        z = split_mm(psum[:, b, :], [(*w0_parts("w3", k), *hid[k]) for k in range(4)], [*bf, w0_marks[-1]])
        for p, _ in hid:
            pairs.give(p, [z])
        gate0.leave()
        done = stt(xs, psum[:, b, :], s3half[:, :], xs, ALU.mult, ALU.add, [z])
        banks.give(b, [done])
        x_ready[c] = [done]
        yield GO

    Q_PART = (0, 0, 1, 0, 2, 1)
    K_PART = (0, 1, 0, 2, 0, 1)
    ROWS_H = 6 * HD
    stack_slots = Slots(list(range(NSTACK)))
    stack_marks = {"readers": ()}
    k_ones = []
    LAG = 2

    def attn_setup():
        t, tf = yield from tiles.take()
        ones_b = t.bitcast(BF16)
        one = dve.do(lambda e: e.memset(ones_b, 1.0), tf)
        cleared = dve.do(lambda e: e.memset(ks_t.bitcast(F32)[:, :, :, :], 0.0))
        cleared = dve.do(lambda e: e.memset(qs_t.bitcast(F32)[:, :, :, :], 0.0))
        d = [dma.do(ks_t[64 * h + ROWS_H:64 * h + ROWS_H + 1, n, h:4:2, :], ones_b[0:2, :], [one, cleared])
             for h in range(2) for n in range(NSTACK)]
        tiles.give(t, d)
        k_ones.extend(d)
        k_ones.append(dve.do(lambda e: e.memset(v_t[:, :, :], 1.0)))
        k_ones.append(dma.do(rope_t[:, :, :], rope))
        k_ones.append(load_native(w0n, n0, []))
        yield GO

    def project_heads(b, half, written):
        c = 2 * b + half
        xn, xm = yield from layernorm(X[:, c * C:(c + 1) * C], x_ready[c])
        where = slice(half * C, half * C + C)
        for side_, (w, ws, bias, bias_s) in enumerate((("q", "qs", "bq", "bqs"), ("k", "ks", "bk", "bks"))):
            turned = []
            for name, bn, table in ((w, bias, 0), (ws, bias_s, 1)):
                bk, bf = yield from banks.take()
                z = full_mm(psum[:, bk, :], [(w0n[:, N0[name]:N0[name] + P], xn, [*xm, *k_ones])], bf)
                t, tf = yield from tiles.take()
                r = stt(t, psum[:, bk, :], col(bn), rope_t[:, table, where], ALU.add, ALU.mult, [z, *tf, *k_ones])
                banks.give(bk, [r])
                turned.append((t, r))
            (t0, r0), (t1, r1) = turned
            full = tt(t0, t0, t1, ALU.add, [r0, r1])
            (p01, f01), (p2, f2) = yield from tiles.take(2)
            hi, mid = p01.bitcast(BF16)[:, 0:C], p01.bitcast(BF16)[:, C:2 * C]
            lo = p2.bitcast(BF16)[:, 0:C]
            m0 = copy_act(hi, t0, [full, *f01])
            rest = tt(t1, t0, hi, ALU.subtract, [m0])
            m1 = copy_act(mid, t1, [rest])
            m2 = tt(lo, t1, mid, ALU.subtract, [m1, *f2])
            tiles.give(t0, [m0, rest])
            tiles.give(t1, [m1, m2])
            d = [dma.do(parts_d[b, side_, 0, :, where], hi, [m0]), dma.do(parts_d[b, side_, 1, :, where], mid, [m1]),
                 dma.do(parts_d[b, side_, 2, :, where], lo, [m2])]
            tiles.give(p01, d[0:2])
            tiles.give(p2, [d[2]])
            written.extend(d)
            yield GO
        yield from attn_gate_v(b)
        bk, bf = yield from banks.take()
        for t in range(TPC):
            z = mm(psum[:, bk, t * TILE:(t + 1) * TILE], xn[:, t * TILE:(t + 1) * TILE],
                   w0n[:, N0["v"]:N0["v"] + P], True, True, [*xm, *bf], t == TPC - 1)
        tiles.give(xn, [z])
        rows_v = v_t[:, half * TPC:(half + 1) * TPC, 0:NH * 9].rearrange("p t (h c) -> p t h c", c=9)
        for t in range(TPC):
            v = tt(rows_v[:, t, :, 0:HD], psum[:, bk, t * TILE:(t + 1) * TILE].rearrange("p (h c) -> p h c", c=HD),
                   rowv[:, ROWS["bv"]:ROWS["bv"] + P].rearrange("p (h c) -> p h c", c=HD), ALU.add,
                   [z, *stack_marks["readers"], *k_ones])
        banks.give(bk, [v])
        written.append(v)
        yield GO

    def attn_gate_v(b):
        while stack_marks.get("done", -1) < b - 1:
            yield

    def attention(b):
        written = []
        for half in range(2):
            yield from project_heads(b, half, written)
        yield from attn_gate_v(b)
        readers = stack_marks["readers"]
        stacks = {}

        def load_stacks(g):
            k_, free = yield from stack_slots.take()
            marks = []
            for h in range(2):
                for side_, order in ((0, Q_PART), (1, K_PART)):
                    for s_, part in enumerate(order):
                        at_ = 64 * h + HD * s_
                        src = parts_d[b, side_, part].rearrange("(j h d) t -> h d j t", h=2, d=HD)[h, :, 2 * g:2 * g + 2]
                        dst = qs_t[at_:at_ + HD, k_, :, :] if side_ == 0 else ks_t[at_:at_ + HD, k_, h:4:2, :]
                        marks.append(dma.do(dst, src, [*written, *free, *k_ones]))
                marks.append(dma.do(qs_t[64 * h + ROWS_H:64 * h + ROWS_H + 1, k_, :, :],
                                    zero.bitcast(BF16).rearrange("p (j t) -> p j t", j=2), [*free, *k_ones]))
            stacks[g] = (k_, marks)
            yield GO

        v_ready = [written[-1]]
        shifts = {}

        def q_of(h, j0, j1):
            return qs_t[:, stacks[h // 4][0], h % 4 // 2, j0:j1]

        def k_of(h, j0, j1):
            return ks_t[:, stacks[h // 4][0], h % 4, j0:j1]

        def find_max(g):
            yield from load_stacks(g)
            mx, mf = yield from tiles.take()
            best = mx[:, 0:32].rearrange("p (h i) -> p h i", h=4)
            marks = []
            for i in range(8):
                wide = (i + 1) * TILE
                per = 4 if i == 0 else 4 if i == 1 else 2 if i < 4 else 1
                for h0 in range(0, 4, per):
                    bk, bf = yield from banks.take_pair()
                    both = psum[:, bk:bk + 2, :].rearrange("p a c -> p (a c)")
                    pitch = wide if per == 4 else C if per == 2 else 0
                    for n in range(per):
                        h = 4 * g + h0 + n
                        for k0 in range(0, wide, C):
                            k1 = min(k0 + C, wide)
                            diag = k1 == wide
                            z = mm(both[:, n * pitch + k0:n * pitch + k1],
                                   q_of(h, i * TILE, (i + 1) * TILE), k_of(h, k0, k1),
                                   True, not diag, [*bf, *stacks[g][1]], False)
                            if diag:
                                z = mm(both[:, n * pitch + k1 - TILE:n * pitch + k1], ident_b, mask_st, False, True,
                                       [], True)
                    view = psum[:, bk:bk + 2, 0:wide] if per == 2 else \
                        both[:, 0:per * wide].rearrange("p (n c) -> p n c", n=per)
                    m = dve.do(lambda e, o=best[:, h0:h0 + per, i], v=view: e.tensor_reduce(o, v, AX.X, ALU.max),
                               [z, *mf])
                    banks.give_pair(bk, [m])
                    marks = [m]
                    yield GO
            bk, bf = yield from banks.take()
            z = mm(psum[0:32, bk, 0:TILE], mx[:, 0:32], ident, True, True, [*marks, *bf], True)
            low = mx[0:32, 64:128].bitcast(BF16)
            n = ts(low, psum[0:32, bk, 0:TILE], -1.0, ALU.mult, [z])
            banks.give(bk, [n])
            d = dma.do(shift_d[b, 4 * g:4 * g + 4].rearrange("h i s -> (h i) s"), low, [n])
            tiles.give(mx, [d])
            shifts[g] = [dma.do(qs_t[64 * h + ROWS_H:64 * h + ROWS_H + 1, stacks[g][0], :, :],
                                shift_d[b, 4 * g:4 * g + 4].rearrange("(j h) i s -> h j (i s)", h=2)[h:h + 1],
                                [d]) for h in range(2)]
            yield GO

        found = []

        def weigh(g):
            while g not in shifts:
                yield
            for half in range(2):
                acc, af = yield from banks.take()
                last = TPC * (half + 1)
                late = []

                def add_rows(i, pr, p, x, q0, n):
                    for n_ in range(2):
                        k = 2 * pr + n_
                        c9 = 9 * (4 * g + k)
                        y = pe.do(lambda e, o=psum[32 * k:32 * k + 32, acc, q0:C], l=v_t[:, i, c9:c9 + 32],
                                  r=p[:, n_, 0:n], st=(i == 0), en=(i == last - 1), k=k:
                                  e.matmul(o, l, r, start=st, stop=en, tile_position=(0, 32 * k)),
                                  [x, *af, *v_ready])
                    twins.give(p, [y])
                    return y

                for i in range(last):
                    q0 = max(0, i * TILE - half * C)
                    n = C - q0
                    for pr in range(2):
                        bk, bf = yield from banks.take_pair()
                        for n_ in range(2):
                            h = 4 * g + 2 * pr + n_
                            diag = i >= TPC * half
                            z = mm(psum[:, bk + n_, 0:n], k_of(h, i * TILE, (i + 1) * TILE),
                                   q_of(h, half * C + q0, half * C + C), True, not diag,
                                   [*bf, *shifts[g]], not diag)
                            if diag:
                                z = mm(psum[:, bk + n_, 0:TILE], ident_b, mask_ts, False, True, [], True)
                        p, pf = yield from twins.take()
                        x = func(ACT.Exp, p[:, :, 0:n], psum[:, bk:bk + 2, 0:n], [z, *pf], scale=HD ** -0.5)
                        banks.give_pair(bk, [x])
                        late.append((i, pr, p, x, q0, n))
                        if len(late) > LAG:
                            y = add_rows(*late.pop(0))
                        yield GO
                while late:
                    y = add_rows(*late.pop(0))
                t, tf = yield from tiles.take()
                m = copy_dve(t, psum[:, acc, :], [y, *tf])
                banks.give(acc, [m])
                found.append((g, half, t, m))
                if half:
                    stack_slots.give(stacks[g][0], [pe.mark()])
                yield GO

        def finish(half):
            mine = [f for f in found if f[1] == half]
            (bn, fn), (bd, fd) = (yield from banks.take()), (yield from banks.take())
            for k, (name, bank, free) in enumerate((("num", bn, fn), ("den", bd, fd))):
                for n_, (g, _, t, m) in enumerate(mine):
                    c0 = MATS[name] + 96 - 32 * g
                    z = mm(psum[:, bank, :], matf[:, c0:c0 + P], t, n_ == 0, n_ == 3, [m, *free], n_ == 3)
            o, of = yield from tiles.take()
            r = dve.do(lambda e: e.reciprocal(o, psum[:, bd, :]), [z, *of])
            a = tt(o, psum[:, bn, :], o, ALU.mult, [r])
            for f in mine:
                tiles.give(f[2], [z])
            z = full_mm(psum[:, bd, :], [(w0n[:, N0["o"]:N0["o"] + P], o, [a])], [r])
            c = 2 * b + half
            xs = X[:, c * C:(c + 1) * C]
            done = stt(xs, psum[:, bd, :], col("bo"), xs, ALU.add, ALU.add, [z])
            tiles.give(o, [z])
            banks.give(bn, [a])
            banks.give(bd, [done])
            x_ready[c] = [done]
            yield GO

        yield from find_max(0)
        for g in range(4):
            searching = find_max(g + 1) if g < 3 else iter(())
            for step in weigh(g):
                yield step
                next(searching, None)
            yield from searching
        stack_marks["readers"] = (pe.mark(),)
        stack_marks["done"] = b
        yield from finish(0)
        yield from finish(1)

    def every(v):
        return v.unsqueeze(2).broadcast_to([P, TPC, E8])

    def gates(number, kind, xn, xm):
        ne = 9 if kind == "l2" else 8
        b, bf = yield from banks.take()
        for t in range(TPC):
            z = mm(psum[:, b, t * ne:(t + 1) * ne], xn[:, t * TILE:(t + 1) * TILE],
                   routerw[:, RW[kind]:RW[kind] + ne], True, True, [*xm, *bf, *need(pe)], t == TPC - 1)
        (r, rf), (o, of) = yield from tiles.take(2)
        logits = psum[:, b, 0:TPC * ne].rearrange("p (t e) -> p t e", e=ne)

        def grid(k):
            return r[:, 32 * k:32 * k + 32].rearrange("p (t e) -> p t e", e=E8)

        def line(k):
            return r[:, 480 + 4 * k:484 + 4 * k]

        def row(name):
            return rowv[:, ROWS[name]:ROWS[name] + E8].unsqueeze(1).broadcast_to([P, TPC, E8])

        def best(v, o_, after):
            return dve.do(lambda e: e.tensor_reduce(o_, v, AX.X, ALU.max), after)

        power = euler[:, 0:32].rearrange("p (t e) -> p t e", e=E8)
        lg = grid(0)
        if kind == "l2":
            m = copy_dve(lg, logits[:, :, 0:E8], [z, *rf, *need(dve)])
            m9 = ts(line(6), logits[:, :, 8], -1.0, ALU.mult, [m])
        else:
            m = tt(lg, logits, row("br1" if kind == "l1" else "br3"), ALU.add, [z, *rf, *need(dve)])
        banks.give(b, [dve.mark()])
        if kind != "l3":
            m = best(lg, line(0), [m])
            m = tt(grid(1), lg, every(line(0)), ALU.subtract, [m])
            m = pool.do(lambda e: e.tensor_tensor(grid(1), power, grid(1), ALU.pow), [m, *need(pool)])
            m = dve.do(lambda e: e.tensor_reduce(line(1), grid(1), AX.X, ALU.add), [m])
            m = dve.do(lambda e: e.reciprocal(line(1), line(1)), [m])
            m = tt(lg, grid(1), every(line(1)), ALU.mult, [m])
        yield GO
        for k, at_ in ((0, 2), (1, 6)):
            src = lg if k == 0 else grid(10)
            top, code, first, mark_ = line(2 + k), grid(at_), line(4), grid(at_ + 1)
            m = best(src, top, [m])
            m = tt(code, src, every(top), ALU.is_equal, [m])
            m = tt(code, code, row("code"), ALU.mult, [m])
            m = best(code, first, [m])
            m = tt(mark_, code, every(first), ALU.is_equal, [m])
            if k == 0:
                m = stt(grid(10), mark_, NEG, lg, ALU.mult, ALU.add, [m])
        one, two = grid(3), grid(7)
        yield GO
        gate = o[:, 0:TPC * ne].rearrange("p (e t) -> p t e", t=TPC)
        if kind == "l1":
            m = stt(one, one, 0.5, lg[:, :, 0:1].broadcast_to([P, TPC, E8]), ALU.mult, ALU.mult, [m])
            m = stt(two, two, 0.5, lg[:, :, 1:2].broadcast_to([P, TPC, E8]), ALU.mult, ALU.mult, [m])
            m = tt(gate, one, two, ALU.add, [m, *of])
        elif kind == "l2":
            m = tt(one, one, two, ALU.add, [m])
            m = stt(gate[:, :, 0:E8], one, 0.5, lg, ALU.mult, ALU.mult, [m, *of])
            m = pool.do(lambda e: e.tensor_tensor(line(6), euler[:, 0:TPC], line(6), ALU.pow), [m, m9])
            m = ts(line(6), line(6), 1.0, ALU.add, [m], 2.0, ALU.mult)
            m = dve.do(lambda e: e.reciprocal(gate[:, :, 8], line(6)), [m])
        else:
            m = tt(line(5), line(3), line(2), ALU.subtract, [m])
            m = pool.do(lambda e: e.tensor_tensor(line(5), euler[:, 0:TPC], line(5), ALU.pow), [m, *need(pool)])
            m = ts(line(6), line(5), 1.0, ALU.add, [m])
            m = dve.do(lambda e: e.reciprocal(line(6), line(6)), [m])
            m = tt(line(5), line(5), line(6), ALU.mult, [m])
            m = tt(one, one, every(line(6)), ALU.mult, [m])
            m = tt(two, two, every(line(5)), ALU.mult, [m])
            m = tt(gate, one, two, ALU.add, [m, *of])
        b, bf = yield from banks.take()
        z = mm(psum[0:TPC * ne, b, 0:TILE], o[:, 0:TPC * ne], ident, True, True, [m, *bf], True)
        tiles.give(r, [m])
        m = copy_dve(o[0:TPC * ne, 128:128 + TILE], psum[0:TPC * ne, b, 0:TILE], [z])
        banks.give(b, [m])
        d = dma.do(gates_d[number, 0:ne * C].rearrange("(r k) -> r k", k=TILE), o[0:TPC * ne, 128:128 + TILE], [m])
        tiles.give(o, [d])
        yield GO
        return d

    def gate_tile(number, e, written):
        t, tf = yield from tiles.take()
        d = dma.do(t, gates_d[number:number + 1, e * C:(e + 1) * C].broadcast_to([P, C]), [written, *tf])
        return t, d

    def weighed(target, marks, bank, y, gate, bias=None):
        t, d = gate
        if bias is None:
            m = tt(t, psum[:, bank, :], t, ALU.mult, [y, d])
        else:
            m = stt(t, psum[:, bank, :], bias, t, ALU.add, ALU.mult, [y, d])
        banks.give(bank, [m])
        a = tt(target, target, t, ALU.add, [m, *marks], pool)
        tiles.give(t, [a])
        return [a]

    def hidden(f, terms, after, **kw):
        b, bf = yield from banks.take()
        z = split_mm(psum[:, b, :], terms, [*bf, *after])
        h, hf = yield from tiles.take()
        a = func(f, h, psum[:, b, :], [z, *hf], **kw)
        banks.give(b, [a])
        p, pf = yield from pairs.take()
        m = split(h, p, [a], pf)
        tiles.give(h, m)
        return p, m, z

    gate_moe = Gate(2)
    w1_marks, w2_marks = [], []

    def parts(w, c0):
        return w[:, 0, c0:c0 + P], w[:, 1, c0:c0 + P]

    def moe1(c, number):
        xs = X[:, c * C:(c + 1) * C]
        xn, xm = yield from layernorm(xs, x_ready[c])
        written = yield from gates(number, "l1", xn, xm)
        yield from gate_moe.enter()
        xp, pf = yield from pairs.take()
        marks = split(xn, xp, xm, pf)
        tiles.give(xn, marks)
        while len(w1_marks) < L1W_COLS // C:
            yield
        for g in range(0, E8, 4):
            hs, gt = [], []
            for e in range(g, g + 4):
                hs.append((yield from hidden(ACT.Relu, [(*parts(w1r, 3 * e * P), xp, marks)], [w1_marks[-1]],
                                             bias=col("l1b1", e))))
            yield GO
            for e in range(g, g + 4):
                p, m, _ = hs[e - g]
                hs[e - g] = yield from hidden(ACT.Relu, [(*parts(w1r, (3 * e + 1) * P), p, m)], [],
                                              bias=col("l1b2", e))
                pairs.give(p, [hs[e - g][2]])
                gt.append((yield from gate_tile(number, e, written)))
            yield GO
            for e in range(g, g + 4):
                p, m, _ = hs[e - g]
                b, bf = yield from banks.take()
                z = split_mm(psum[:, b, :], [(*parts(w1r, (3 * e + 2) * P), p, m)], bf)
                pairs.give(p, [z])
                x_ready[c] = weighed(xs, x_ready[c], b, z, gt[e - g], col("l1b3", e))
            yield GO
        pairs.give(xp, [z])
        gate_moe.leave()

    def moe2(c, number):
        xs = X[:, c * C:(c + 1) * C]
        xn, xm = yield from layernorm(xs, x_ready[c])
        written = yield from gates(number, "l2", xn, xm)
        yield from gate_moe.enter()
        xp, pf = yield from pairs.take()
        marks = split(xn, xp, xm, pf)
        tiles.give(xn, marks)
        while len(w2_marks) < -(-L2W_COLS // C):
            yield
        for g in range(0, 9, 3):
            hs, gt = [], []
            for e in range(g, g + 3):
                if e < E8:
                    hs.append((yield from hidden(ACT.Silu, [(*parts(w2r, 2 * e * P), xp, marks)], [w2_marks[-1]])))
                else:
                    (b1, f1), (b2, f2) = (yield from banks.take()), (yield from banks.take())
                    zg = split_mm(psum[:, b1, :], [(*parts(w2r, L2W_GU), xp, marks)], f1)
                    zu = split_mm(psum[:, b2, :], [(*parts(w2r, L2W_GU + P), xp, marks)], f2)
                    h, hf = yield from tiles.take()
                    a = func(ACT.Silu, h, psum[:, b1, :], [zg, *hf])
                    banks.give(b1, [a])
                    a = tt(h, psum[:, b2, :], h, ALU.mult, [zu, a])
                    banks.give(b2, [a])
                    p, pf = yield from pairs.take()
                    m = split(h, p, [a], pf)
                    tiles.give(h, m)
                    hs.append((p, m, zu))
                gt.append((yield from gate_tile(number, e, written)))
            yield GO
            for e in range(g, g + 3):
                p, m, _ = hs[e - g]
                b, bf = yield from banks.take()
                w = (2 * e + 1) * P if e < E8 else L2W_DOWN
                z = split_mm(psum[:, b, :], [(*parts(w2r, w), p, m)], bf)
                pairs.give(p, [z])
                x_ready[c] = weighed(xs, x_ready[c], b, z, gt[e - g])
            yield GO
        pairs.give(xp, [z])
        gate_moe.leave()

    slots3 = Slots([])
    loaded3, users3 = {}, {}

    def stream3(number):
        for u in range(NC_ // 2):
            for e in range(E8):
                k, kf = yield from slots3.take()
                marks = []
                yield from load_split(w3r[:, k, :, :], w3[e], L3W_COLS, kf, marks)
                loaded3[number, u, e] = (k, marks)

    def moe3(c, number):
        xs = X[:, c * C:(c + 1) * C]
        xn, xm = yield from layernorm(xs, x_ready[c])
        written = yield from gates(number, "l3", xn, xm)
        yield from gate_moe.enter()
        xp, pf = yield from pairs.take()
        marks = split(xn, xp, xm, pf)
        total = [*xm, *marks]
        for e in range(E8):
            key = (number // NC_, c // 2, e)
            while key not in loaded3:
                yield
            k, wm = loaded3[key]
            gt = yield from gate_tile(number, e, written)
            while len(pairs.free) < 4:
                yield
            hs = []
            for f in range(4):
                hs.append((yield from hidden(ACT.Relu, [(*parts(w3r[:, k, :, :], f * P), xp, marks)], wm,
                                             bias=col("l3b1", 4 * e + f))))
            yield GO
            b, bf = yield from banks.take()
            z = split_mm(psum[:, b, :], [(*parts(w3r[:, k, :, :], (4 + f) * P), hs[f][0], hs[f][1]) for f in range(4)],
                         bf)
            for h in hs:
                pairs.give(h[0], [z])
            users3[key] = users3.get(key, ()) + (z,)
            if len(users3[key]) == 2:
                slots3.give(k, users3[key])
            total = weighed(xn, total, b, z, gt, col("l3b2", e))
            yield GO
        pairs.give(xp, [z])
        gate_moe.leave()
        y, ym = yield from layernorm(xn, total, col("l3g"), col("l3be"))
        tiles.give(xn, ym)
        done = stt(xs, y, 0.5, xs, ALU.mult, ALU.add, [*ym, *x_ready[c]])
        tiles.give(y, [done])
        x_ready[c] = [done]
        yield GO

    n_marks = []

    def open_b():
        before = [q.mark() for q in (pe, act, dve, pool)]
        n_marks.extend([load_native(w1n, n1, before), load_native(w2n, n2, before), load_native(w3n, n3, before)])
        a = func(ACT.Exp, neg_a[:, :], colv[:, COLS["m2A"]:COLS["m2A"] + 16], need(act))
        n_marks.append(dve.do(lambda e: e.memset(ones[:, :], 1.0), before))
        n_marks.append(ts(neg_a[:, :], neg_a[:, :], -1.0, ALU.mult, [a]))
        for i in range(EXTRA):
            tiles.give(extra[:, i, :], before)
        yield GO

    def load_b():
        before = [q.mark() for q in (pe, act, dve, pool)]
        yield from load_split(w1r, w1, L1W_COLS, before, w1_marks)
        yield from load_split(w2r, w2, L2W_COLS, before, w2_marks)

    def close_extra():
        freed = []
        while len(freed) < EXTRA:
            for x in list(tiles.free):
                if x[0].tensor.name == extra.name:
                    tiles.free.remove(x)
                    freed.append(x[1])
            if len(freed) < EXTRA:
                yield
        for k in range(NEXP):
            slots3.give(k, [t for f in freed for t in f])
        yield GO

    def softplus(z, bank, bias, after):
        (a, af), (m, mf) = yield from tiles.take(2)
        x = func(ACT.Abs, a, psum[:, bank, :], [*after, *af], bias=bias)
        y = ts(m, psum[:, bank, :], bias, ALU.add, [*after, x, *mf], 0.0, ALU.max)
        banks.give(bank, [x, y])
        x = func(ACT.Exp, a, a, [x], scale=-1.0)
        return a, m, [x, y]

    tail_marks = {}
    gate_m = Gate(2)

    def mamba1(c):
        xs = X[:, c * C:(c + 1) * C]
        yield from gate_m.enter()
        xn, xm = yield from layernorm(xs, x_ready[c])
        later = c % 2 == 1
        while later and (1, c - 1) not in tail_marks:
            yield
        xc, sz = [], []
        for blk in range(2):
            b, bf = yield from banks.take()
            w0_ = N1["in"] + blk * P
            z = full_mm(psum[:, b, :], [(w1n[:, w0_:w0_ + P], xn, [*xm, *n_marks])], bf)
            t, tf = yield from tiles.take()
            v = psum[:, b, :]
            tail = copy_act(tails[:, c, blk, 0:3], v[:, C - 3:C], [z])
            m = ts(t, v, col("m1conv", 6 + blk), ALU.mult, [z, tail, *tf])
            for d in range(1, 4):
                w = col("m1conv", 2 * (3 - d) + blk)
                m = stt(t[:, d:C], v[:, 0:C - d], w, t[:, d:C], ALU.mult, ALU.add, [m])
                if later:
                    m = stt(t[:, 0:d], tails[:, c - 1, blk, 3 - d:3], w, t[:, 0:d], ALU.mult, ALU.add,
                            [m, *tail_marks[1, c - 1]])
            banks.give(b, [tail, m])
            tail_marks.setdefault((0, c), []).append(tail)
            xc.append((t, func(ACT.Silu, t, t, [m], bias=col("m1cb", blk))))
        tail_marks[1, c] = tail_marks[0, c]
        for blk in range(2):
            b, bf = yield from banks.take()
            w0_ = N1["in"] + (2 + blk) * P
            z = full_mm(psum[:, b, :], [(w1n[:, w0_:w0_ + P], xn, xm)], bf)
            t, tf = yield from tiles.take()
            a = func(ACT.Silu, t, psum[:, b, :], [z, *tf])
            banks.give(b, [a])
            sz.append((t, a))
        tiles.give(xn, [z])
        yield GO
        sp = []
        for o in range(2):
            b, bf = yield from banks.take()
            z = full_mm(psum[:, b, :], [(w1n[:, N1["dt"] + k * 2 * P + o * P:N1["dt"] + k * 2 * P + (o + 1) * P], xc[k][0],
                                         [xc[k][1]]) for k in range(2)], bf)
            sp.append((yield from softplus(z, b, col("m1dtb", o), [z])))
        dt = []
        for o in range(2):
            a, m, marks = sp[o]
            x = func(ACT.Ln, a, a, marks, bias=1.0)
            y = tt(m, a, m, ALU.add, [x, *marks])
            y = tt(m, m, xc[o][0], ALU.mult, [y])
            tiles.give(a, [y])
            dt.append((m, y))
        yield GO
        (b, bf), (bt, tf), (ct, cf) = (yield from banks.take()), (yield from tiles.take()), (yield from tiles.take())
        for k in range(2):
            for half in range(2):
                c0 = N1["x"] + k * 32 + half * 16
                z = pe.do(lambda e, o=psum[32 * half:32 * half + 16, b, :], l=w1n[:, c0:c0 + 16], r=xc[k][0], k=k, h=half:
                          e.matmul(o, l, r, start=(k == 0), stop=(k == 1), tile_position=(0, 32 * h)), bf)
        m = copy_act(bt[0:16, :], psum[0:16, b, :], [z, *tf])
        m = tt(ct[0:16, :], psum[32:48, b, :], bt[0:16, :], ALU.mult, [m, *cf])
        tiles.give(bt, [m])
        banks.give(b, [m])
        (bs, fs), (bg, fg) = (yield from banks.take()), (yield from banks.take())
        s_ = full_mm(psum[:, bs, :], [(ones[:, :], dt[o][0], [dt[o][1]]) for o in range(2)], fs)
        g_ = mm(psum[:, bg, :], ones[0:16, :], ct[0:16, :], True, True, [m, *fg], True)
        for t, _ in dt:
            tiles.give(t, [s_])
        g, gf = yield from tiles.take()
        tiles.give(ct, [g_])
        m = copy_act(g, psum[:, bg, :], [g_, *gf])
        banks.give(bg, [m])
        m = tt(g, psum[:, bs, :], g, ALU.mult, [m, s_])
        banks.give(bs, [m])
        ys = []
        for k in range(2):
            t = xc[k][0]
            y = stt(t, t, col("m1D", k), g, ALU.mult, ALU.add, [m, z])
            y = tt(t, t, sz[k][0], ALU.mult, [y, sz[k][1]])
            tiles.give(sz[k][0], [y])
            ys.append((w1n[:, N1["o"] + k * P:N1["o"] + (k + 1) * P], t, [y]))
        tiles.give(g, [y])
        yield GO
        b, bf = yield from banks.take()
        z = full_mm(psum[:, b, :], ys, bf)
        for k in range(2):
            tiles.give(xc[k][0], [z])
        done = tt(xs, psum[:, b, :], xs, ALU.add, [z])
        banks.give(b, [done])
        x_ready[c] = [done]
        gate_m.leave()
        yield GO

    state_marks = {}

    def mamba2(c):
        xs = X[:, c * C:(c + 1) * C]
        yield from gate_m.enter()
        src, sm = yield from layernorm(xs, x_ready[c])
        hn, hm = yield from layernorm(src, sm, col("n1g"), col("n1b"))
        later = c % 2 == 1
        while later and (2, c - 1) not in tail_marks:
            yield
        b, bf = yield from banks.take()
        z = full_mm(psum[:, b, :], [(w2n[:, 0:P], hn, [*hm, *n_marks])], bf)
        xc, tf = yield from tiles.take()
        v = psum[:, b, :]
        tail = copy_act(tails[:, c, 0, 3:4], v[:, C - 1:C], [z])
        m = ts(xc, v, col("m2conv", 1), ALU.mult, [z, tail, *tf])
        m = stt(xc[:, 1:C], v[:, 0:C - 1], col("m2conv", 0), xc[:, 1:C], ALU.mult, ALU.add, [m])
        if later:
            m = stt(xc[:, 0:1], tails[:, c - 1, 0, 3:4], col("m2conv", 0), xc[:, 0:1], ALU.mult, ALU.add,
                    [m, tail_marks[2, c - 1]])
        banks.give(b, [tail, m])
        tail_marks[2, c] = tail
        xm = func(ACT.Silu, xc, xc, [m], bias=col("m2cb"))
        b, bf = yield from banks.take()
        z = full_mm(psum[:, b, :], [(w2n[:, P:2 * P], hn, hm)], bf)
        tiles.give(hn, [z])
        sz, zf = yield from tiles.take()
        szm = func(ACT.Silu, sz, psum[:, b, :], [z, *zf])
        banks.give(b, [szm])
        yield GO
        b, bf = yield from banks.take()
        z = mm(psum[0:64, b, :], w2n[:, N2["xdt"]:N2["xdt"] + 64], xc, True, True, [xm, *bf], True)
        d64, df = yield from tiles.take()
        dm = copy_act(d64[0:64, :], psum[0:64, b, :], [z, *df])
        banks.give(b, [dm])
        b, bf = yield from banks.take()
        z = mm(psum[0:96, b, :], w2n[:, N2["xbc"]:N2["xbc"] + 96], xc, True, True, [xm, *bf], True)
        (bc, f1), (rest, f2) = yield from tiles.take(2)
        bcb = bc.bitcast(BF16)[:, 0:C]
        m = copy_act(bcb[0:96, :], psum[0:96, b, :], [z, *f1])
        m = tt(rest[0:96, :], psum[0:96, b, :], bcb[0:96, :], ALU.subtract, [m, *f2])
        banks.give(b, [m])
        for r0 in (32, 64):
            m1 = copy_act(bcb[r0:r0 + 32, :], rest[r0:r0 + 32, :], [m])
        m = tt(rest[64:96, :], rest[64:96, :], bcb[64:96, :], ALU.subtract, [m1])
        bcm = copy_act(bcb[64:96, :], rest[64:96, :], [m])
        tiles.give(rest, [bcm])
        b, bf = yield from banks.take()
        z = mm(psum[:, b, :], w2n[0:64, N2["dt"]:N2["dt"] + P], d64[0:64, :], True, True, [dm, *bf], True)
        tiles.give(d64, [z])
        a, dl, marks = yield from softplus(z, b, col("m2dtb"), [z])
        x = func(ACT.Ln, a, a, marks, bias=1.0)
        dlm = tt(dl, a, dl, ALU.add, [x, *marks])
        um = tt(a, dl, xc, ALU.mult, [dlm, xm])
        u = a
        yield GO
        by, yf = yield from banks.take()
        late = []

        def add_state(n, t, m):
            y = mm(psum[:, by, :], ident, t, n == 0, n == NS - 1, [m, *yf], True)
            tiles.give(t, [y])
            return y

        for n in range(NS):
            while later and (c - 1, n) not in state_marks:
                yield
            (bb, f1), (bc_, f2) = (yield from banks.take()), (yield from banks.take())
            zb = mm(psum[:, bb, :], pickb[:, n:n + 1].broadcast_to([96, P]), bcb[0:96, :], True, True, [bcm, *f1], True)
            zc = mm(psum[:, bc_, :], pickb[:, NS + n:NS + n + 1].broadcast_to([96, P]), bcb[0:96, :], True, True,
                    f2, True)
            (da, g1), (db, g2) = yield from tiles.take(2)
            m1 = func(ACT.Exp, da, dl, [dlm, *g1], scale=neg_a[:, n:n + 1])
            m2 = tt(db, psum[:, bb, :], u, ALU.mult, [zb, um, *g2])
            banks.give(bb, [m2])
            start, wait = (states[:, c // 2, n:n + 1], [state_marks[c - 1, n]]) if later else (0.0, [])
            h = dve.do(lambda e, o=da, d0=da, d1=db, i=start: e.tensor_tensor_scan(o, d0, d1, i, ALU.mult, ALU.add),
                       [m1, m2, *wait])
            if not later:
                state_marks[c, n] = pool.do(lambda e, o=states[:, c // 2, n:n + 1], i=da[:, C - 1:C]:
                                            e.tensor_copy(o, i), [h])
            m = copy_act(db, psum[:, bc_, :], [zc, h])
            banks.give(bc_, [m])
            m = tt(db, db, da, ALU.mult, [m, h], pool)
            tiles.give(da, [m])
            late.append((n, db, m))
            if len(late) > 2:
                add_state(*late.pop(0))
            yield GO
        while late:
            y = add_state(*late.pop(0))
        tiles.give(bc, [zc])
        tiles.give(dl, [m1])
        tiles.give(u, [m2])
        m = stt(xc, xc, col("m2D"), psum[:, by, :], ALU.mult, ALU.add, [y])
        banks.give(by, [m])
        m = tt(xc, xc, sz, ALU.mult, [m, szm])
        b, bf = yield from banks.take()
        z = full_mm(psum[:, b, :], [(w2n[:, N2["o"]:N2["o"] + P], xc, [m])], bf)
        tiles.give(xc, [z])
        m = copy_act(sz, psum[:, b, :], [z, m])
        banks.give(b, [m])
        yn, ym = yield from layernorm(sz, [m], col("mg"), col("mb"))
        tiles.give(sz, ym)
        sm = [tt(src, src, yn, ALU.add, [*ym, *sm])]
        tiles.give(yn, sm)
        fn, fm = yield from layernorm(src, sm, col("n2g"), col("n2b"))
        hid = []
        for o in range(4):
            b, bf = yield from banks.take()
            z = full_mm(psum[:, b, :], [(w2n[:, N2["f1"] + o * P:N2["f1"] + (o + 1) * P], fn, fm)], bf)
            t, tf = yield from tiles.take()
            m = func(ACT.Copy, t, psum[:, b, :], [z, *tf], scale=0.01)
            m = tt(t, psum[:, b, :], t, ALU.max, [m])
            banks.give(b, [m])
            hid.append((w2n[:, N2["f2"] + o * P:N2["f2"] + (o + 1) * P], t, [m]))
        tiles.give(fn, [z])
        yield GO
        b, bf = yield from banks.take()
        z = full_mm(psum[:, b, :], hid, bf)
        for _, t, _ in hid:
            tiles.give(t, [z])
        sm = [tt(src, psum[:, b, :], src, ALU.add, [z, *sm])]
        banks.give(b, sm)
        fn, fm = yield from layernorm(src, sm, col("n3g"), col("n3b"))
        b, bf = yield from banks.take()
        z = full_mm(psum[:, b, :], [(w2n[:, N2["fe"]:N2["fe"] + P], fn, fm)], bf)
        tiles.give(fn, [z])
        m = stt(src, psum[:, b, :], col("feb"), src, ALU.add, ALU.add, [z, *sm])
        banks.give(b, [m])
        done = tt(xs, xs, src, ALU.add, [m])
        tiles.give(src, [done])
        x_ready[c] = [done]
        gate_m.leave()
        yield GO

    gate_l = Gate(1)

    def positive(bank, z):
        t, tf = yield from tiles.take()
        m = ts(t, psum[:, bank, :], 0.0, ALU.min, [z, *tf])
        m = func(ACT.Exp, t, t, [m])
        m = stt(t, psum[:, bank, :], 0.0, t, ALU.max, ALU.add, [m])
        banks.give(bank, [m])
        return t, m

    def linear_attention(b_):
        yield from gate_l.enter()
        xn = []
        for half in range(2):
            c = 2 * b_ + half
            xn.append((yield from layernorm(X[:, c * C:(c + 1) * C], x_ready[c])))
        (bkv, fkv), (bks, fks) = (yield from banks.take()), (yield from banks.take())
        for half in range(2):
            x_, xm = xn[half]
            toks = []
            for name in ("k", "v"):
                b, bf = yield from banks.take()
                for t in range(TPC):
                    z = mm(psum[:, b, t * TILE:(t + 1) * TILE], x_[:, t * TILE:(t + 1) * TILE],
                           w3n[:, N3[name]:N3[name] + P], True, True, [*xm, *bf, *n_marks], t == TPC - 1)
                if name == "k":
                    toks.append((yield from positive(b, z)))
                else:
                    t_, tf = yield from tiles.take()
                    m = copy_act(t_, psum[:, b, :], [z, *tf])
                    banks.give(b, [m])
                    toks.append((t_, m))
            (kt, km), (vt, vm) = toks
            for t in range(TPC):
                first, last = half == 0 and t == 0, half == 1 and t == TPC - 1
                sl = slice(t * TILE, (t + 1) * TILE)
                mm(psum[:, bkv, 0:P], kt[:, sl], vt[:, sl], first, last, [km, vm, *fkv])
                z = mm(psum[:, bks, 0:P], kt[:, sl], ones[:, :], first, last, fks, t == TPC - 1)
            tiles.give(kt, [z])
            tiles.give(vt, [z])
            yield GO
        st, sf = yield from tiles.take()
        m = tt(st[:, 0:P], psum[:, bkv, 0:P], heads, ALU.mult, [z, *sf])
        m = tt(st[:, P:2 * P], psum[:, bks, 0:P], heads, ALU.mult, [z, m])
        banks.give(bkv, [m])
        banks.give(bks, [m])
        yield GO
        outs = []
        for half in range(2):
            x_, xm = xn[half]
            b, bf = yield from banks.take()
            z = full_mm(psum[:, b, :], [(w3n[:, N3["q"]:N3["q"] + P], x_, xm)], bf)
            q, qm = yield from positive(b, z)
            (bn, fn), (bd, fd) = (yield from banks.take()), (yield from banks.take())
            zn = full_mm(psum[:, bn, :], [(st[:, 0:P], q, [qm, m])], fn)
            zd = full_mm(psum[:, bd, :], [(st[:, P:2 * P], q, [])], fd)
            d = ts(q, psum[:, bd, :], 1e-6, ALU.max, [zd, zn])
            banks.give(bd, [d])
            d = dve.do(lambda e, q=q: e.reciprocal(q, q), [d])
            d = tt(q, psum[:, bn, :], q, ALU.mult, [d, zn])
            banks.give(bn, [d])
            loc, lf = yield from tiles.take()
            l_ = ts(loc, x_, col("c3w", 1), ALU.mult, [*xm, *lf], col("c3b"), ALU.add)
            l_ = stt(loc[:, 1:C], x_[:, 0:C - 1], col("c3w", 0), loc[:, 1:C], ALU.mult, ALU.add, [l_])
            l_ = stt(loc[:, 0:C - 1], x_[:, 1:C], col("c3w", 2), loc[:, 0:C - 1], ALU.mult, ALU.add, [l_])
            other, om = xn[1 - half]
            if half:
                l_ = stt(loc[:, 0:1], other[:, C - 1:C], col("c3w", 0), loc[:, 0:1], ALU.mult, ALU.add, [l_, *om])
            else:
                l_ = stt(loc[:, C - 1:C], other[:, 0:1], col("c3w", 2), loc[:, C - 1:C], ALU.mult, ALU.add, [l_, *om])
            l_ = tt(loc, loc, q, ALU.add, [l_, d])
            tiles.give(q, [l_])
            outs.append((loc, l_))
            yield GO
        tiles.give(st, [zd])
        for half in range(2):
            tiles.give(xn[half][0], [outs[1][1], z])
        for half in range(2):
            loc, l_ = outs[half]
            c = 2 * b_ + half
            xs = X[:, c * C:(c + 1) * C]
            b, bf = yield from banks.take()
            z = full_mm(psum[:, b, :], [(w3n[:, N3["p"]:N3["p"] + P], loc, [l_])], bf)
            tiles.give(loc, [z])
            done = stt(xs, psum[:, b, :], col("bp"), xs, ALU.add, ALU.add, [z])
            banks.give(b, [done])
            x_ready[c] = [done]
        gate_l.leave()
        yield GO


    jobs = []
    jobs.append(("w0", lambda: load_split(w0r, w0, L0W_COLS, [], w0_marks), []))
    for c in range(NC_):
        jobs.append((("ffn0", c), lambda c=c: ffn0(c), []))
    jobs.append(("attn_setup", attn_setup, []))
    for b in range(NB):
        if LAST >= 2:
            jobs.append((("attn0", b), lambda b=b: attention(b), ["attn_setup", ("ffn0", 2 * b), ("ffn0", 2 * b + 1)]))
    if LAST >= 3:
        for c in range(NC_):
            jobs.append((("ffn0b", c), lambda c=c: ffn0(c), [("attn0", c // 2)]))
    last = [("ffn0b", c) for c in range(NC_)]

    def stage(n, name, make, order=range(NC_), before=(), per=1):
        nonlocal last
        if LAST < n:
            return
        for i in order:
            deps = [last[c] for c in range(per * i, per * (i + 1))]
            jobs.append(((name, i), lambda i=i: make(i), [*deps, *before]))
        last = [(name, c // per) for c in range(NC_)]

    across = (0, 2, 4, 6, 1, 3, 5, 7)
    if LAST >= 4:
        jobs.append(("load_b", load_b, [("attn0", b) for b in range(NB)]))
        jobs.append(("open_b", open_b, list(last)))
    stage(4, "moe1", lambda c: moe1(c, c), before=["open_b"])
    stage(5, "mamba1", mamba1, across)
    stage(6, "moe1b", lambda c: moe1(c, NC_ + c))
    stage(7, "moe2", lambda c: moe2(c, 2 * NC_ + c))
    stage(8, "mamba2", mamba2, across)
    stage(9, "moe2b", lambda c: moe2(c, 3 * NC_ + c))
    if LAST >= 10:
        jobs.append(("close_extra", close_extra, list(last)))
        jobs.append(("stream3", lambda: stream3(4), ["close_extra"]))
    stage(10, "moe3", lambda c: moe3(c, 4 * NC_ + c))
    stage(11, "attn3", linear_attention, range(NB), per=2)
    if LAST >= 12:
        jobs.append(("stream3b", lambda: stream3(5), ["stream3"]))
    stage(12, "moe3b", lambda c: moe3(c, 5 * NC_ + c))
    run_jobs(jobs, 4)

    ends = [dma.do(out[:, c * C:(c + 1) * C], X[:, c * C:(c + 1) * C], x_ready[c]) for c in range(NC_)]

    with nc.Block() as block:
        @block.sync
        def _(eng):
            dma.replay(eng)
            for i, sem in enumerate(dma.sems):
                turns = (dma.n - i + len(dma.sems) - 1) // len(dma.sems)
                if turns > 0:
                    eng.wait_ge(sem, 16 * turns)

        @block.tensor
        def _(eng):
            pe.replay(eng)

        @block.scalar
        def _(eng):
            act.replay(eng)

        @block.vector
        def _(eng):
            dve.replay(eng)

        @block.gpsimd
        def _(eng):
            pool.replay(eng)


def kernel(**inputs):
    import numpy as np
    import concourse.bacc as bacc
    from concourse.bass_utils import run_bass_kernel_spmd

    g = {k: np.asarray(v) for k, v in inputs.items()}

    def lhs(w):
        o, i = w.shape
        k = -(-i // P)
        full = np.zeros((k * P, o), w.dtype)
        full[:i] = w.T
        return full.reshape(k, P, o).transpose(1, 0, 2).reshape(P, k * o)

    def side(*parts):
        return np.ascontiguousarray(np.concatenate(parts, axis=1))

    def columns(v):
        return np.asarray(v).reshape(-1, P).T

    swap = np.arange(P) ^ 1
    wq, wk, wv = np.split(g["L0_attn_w_qkv"], 3)
    bq, bk, bv = np.split(g["L0_attn_b_qkv"], 3)
    packed = {
        "x_t": g["L0_attn_x"].reshape(T, P).T,
        "w0": side(lhs(g["L0_ffn_w1_w"]), lhs(g["L0_ffn_w2_w"]), lhs(g["L0_ffn_h1_w"]), lhs(g["L0_ffn_h2_w"]),
                   lhs(g["L0_ffn_w3_w"])),
        "w1": side(*[g[f"L1_ffn_w{k}"][e] for e in range(E8) for k in (1, 2, 3)]),
        "w2": side(*[g[f"L2_ffn_w{k}"][e] for e in range(E8) for k in (1, 2)],
                   g["L2_ffn_shared_gate_up"], g["L2_ffn_shared_down"]),
        "w3": np.stack([side(lhs(g["L3_ffn_W1"][e]), lhs(g["L3_ffn_W2"][e])) for e in range(E8)]),
        "n0": side(lhs(wq), lhs(wq[swap]), lhs(wk), lhs(wk[swap]), lhs(wv), lhs(g["L0_attn_w_out"])),
        "n1": side(lhs(g["L1_attn_in_proj_w"]), lhs(g["L1_attn_dt_proj_w"]), lhs(g["L1_attn_x_proj_w"]),
                   lhs(g["L1_attn_out_proj_w"])),
        "n2": side(lhs(g["L2_attn_in_proj_w"]), lhs(g["L2_attn_x_proj_w"][:64]),
                   *[lhs(g["L2_attn_x_proj_w"][64:])] * 3, lhs(g["L2_attn_dt_proj_w"]),
                   lhs(g["L2_attn_out_proj_w"]), lhs(g["L2_attn_ffn_w1"]), lhs(g["L2_attn_ffn_w2"]),
                   lhs(g["L2_attn_fe_w"])),
        "n3": side(*[lhs(g[f"L3_attn_W{k}"]) for k in "qkvp"]),
        "rw": side(g["L1_ffn_gate_w"].T, g["L2_ffn_router_w"], g["L2_ffn_shared_gate_w"], g["L3_ffn_Wr"].T),
    }
    cols = {"s1": g["L0_ffn_w1_s"], "s2": g["L0_ffn_w2_s"], "h1s": g["L0_ffn_h1_s"], "h2s": g["L0_ffn_h2_s"],
            "w3s": g["L0_ffn_w3_s"], "bq": bq, "bqs": bq[swap], "bk": bk, "bks": bk[swap], "bo": g["L0_attn_b_out"],
            "l1b1": g["L1_ffn_b1"], "l1b2": g["L1_ffn_b2"], "l1b3": g["L1_ffn_b3"],
            "m1conv": g["L1_attn_conv_w"][:, 0, :].T, "m1cb": g["L1_attn_conv_b"], "m1dtb": g["L1_attn_dt_proj_b"],
            "m1D": g["L1_attn_D_param"], "m2conv": g["L2_attn_conv_w"].T, "m2cb": g["L2_attn_conv_b"],
            "m2dtb": g["L2_attn_dt_proj_b"], "m2D": g["L2_attn_Dp"], "m2A": g["L2_attn_A_log"].T,
            "mg": g["L2_attn_mnorm_g"], "mb": g["L2_attn_mnorm_b"], "n1g": g["L2_attn_n1_g"], "n1b": g["L2_attn_n1_b"],
            "n2g": g["L2_attn_n2_g"], "n2b": g["L2_attn_n2_b"], "n3g": g["L2_attn_n3_g"], "n3b": g["L2_attn_n3_b"],
            "feb": g["L2_attn_fe_b"], "c3w": g["L3_attn_conv_w"].T, "c3b": g["L3_attn_conv_b"], "bp": g["L3_attn_bp"],
            "l3b1": g["L3_ffn_b1"], "l3b2": g["L3_ffn_b2"], "l3g": g["L3_ffn_gamma"], "l3be": g["L3_ffn_beta"]}
    packed["cols"] = side(*[columns(np.ascontiguousarray(cols[k])) for k in COLS])
    f = np.float32
    packed["rows"] = np.concatenate([g["L1_ffn_gate_b"], g["L3_ffn_br"], np.arange(8, 0, -1).astype(f), bv])[None, :]
    i, j = np.arange(P)[:, None], np.arange(P)[None, :]
    band = np.arange(224)[None, :]
    num = (i % 32 < 8) & (band == 96 + 8 * (i // 32) + i % 32)
    den = (i % 32 == 8) & (band >= 96 + 8 * (i // 32)) & (band < 104 + 8 * (i // 32))
    packed["mats"] = side((i == j).astype(f), (i // HD == j // HD).astype(f), num.astype(f), den.astype(f),
                          ((i == j) - f(1 / P)).astype(f), np.where(j > i, f(NEG), f(0)), np.where(j < i, f(NEG), f(0)),
                          ((i % 32 == np.arange(32)) & (i < 96)).astype(f))
    dims = np.arange(0, HD, 2, dtype=f)
    inv = (f(1) / f(10000.0) ** (dims / f(HD))).astype(f)
    ang = np.arange(S, dtype=f)[:, None] * inv[None, :]
    feat = np.arange(P)
    cos, sin = np.cos(ang).astype(f)[:, feat % HD // 2].T, np.sin(ang).astype(f)[:, feat % HD // 2].T
    packed["rope"] = np.stack([cos, np.where(feat % 2, f(1), f(-1))[:, None] * sin], axis=1)

    packed["zero"] = np.zeros((1, S), f)

    nc = bacc.Bacc("TRN2", target_bir_lowering=False, num_devices=1)
    arrays, args = {}, {}
    for name, a in packed.items():
        a = np.ascontiguousarray(a)
        arrays[f"in_{name}"] = a
        args[name] = nc.dram_tensor(f"in_{name}", a.shape, F32, kind="ExternalInput").ap()
    args["rows"] = args["rows"].broadcast_to([P, NROWS])
    args["out"] = nc.dram_tensor("out_x", (P, T), F32, kind="ExternalOutput").ap()
    build(nc, **args)
    r = run_bass_kernel_spmd(nc, [arrays], core_ids=[0])
    return np.ascontiguousarray(r.results[0]["out_x"].T).reshape(NB, S, P)
```

```python
import concourse.bass as bass
from concourse import mybir

P = 128
T = 4096
NB, S = 4, 1024
C = 512
NC_ = T // C
TILE = 128
TPC = C // TILE
NH, HD = 16, 8
E8 = 8
NEG = -1e30
EPS = 1e-5
EULER = 2.718281828459045

F32, F32R, BF16 = mybir.dt.float32, mybir.dt.float32r, mybir.dt.bfloat16
ALU = mybir.AluOpType
ACT = mybir.ActivationFunctionType
AX = mybir.AxisListType

L0W = {"w1": 0, "w2": 512, "h1": 1024, "h2": 1024 + 2048, "w3": 1024 + 4096}
L0W_COLS = 1024 + 4096 + 512
L1W_COLS = E8 * 3 * P
L2W_GU, L2W_DOWN = E8 * 2 * P, E8 * 2 * P + 2 * P
L2W_COLS = L2W_DOWN + P
L3W_COLS = 8 * P
N0 = {"q": 0, "qs": 128, "k": 256, "ks": 384, "v": 512, "o": 640}
N0_COLS = 768
N1 = {"in": 0, "dt": 512, "x": 1024, "o": 1088}
N1_COLS = 1344
N2 = {"in": 0, "xdt": 256, "xbc": 320, "dt": 416, "o": 544, "f1": 672, "f2": 1184, "fe": 1696}
N2_COLS = 1824
N3 = {"q": 0, "k": 128, "v": 256, "p": 384}
N3_COLS = 512

_at = 0
COLS = {}
for _name, _n in [("s1", 4), ("s2", 4), ("h1s", 4), ("h2s", 4), ("w3s", 1),
                  ("bq", 1), ("bqs", 1), ("bk", 1), ("bks", 1), ("bo", 1),
                  ("l1b1", 8), ("l1b2", 8), ("l1b3", 8),
                  ("m1conv", 8), ("m1cb", 2), ("m1dtb", 2), ("m1D", 2),
                  ("m2conv", 2), ("m2cb", 1), ("m2dtb", 1), ("m2D", 1), ("m2A", 16),
                  ("mg", 1), ("mb", 1), ("n1g", 1), ("n1b", 1), ("n2g", 1), ("n2b", 1), ("n3g", 1), ("n3b", 1),
                  ("feb", 1), ("c3w", 3), ("c3b", 1), ("bp", 1),
                  ("l3b1", 32), ("l3b2", 8), ("l3g", 1), ("l3be", 1)]:
    COLS[_name] = _at
    _at += _n
NCOLS = _at
ROWS = {"br1": 0, "br3": 8, "code": 16, "bv": 24}
NROWS = 24 + P
MATS = {"ident": 0, "heads": 128, "num": 256, "den": 480, "centre": 704, "mask_st": 832, "mask_ts": 960, "pick": 1088}
KEPT_MATS = 704
NMATS = 1088 + 32
RW = {"l1": 0, "l2": 8, "l3": 17}
NRW = 25


class Token:

    def __init__(self, sem, value, time):
        self.sem, self.value, self.time = sem, value, time


def waits_of(queue, after):
    waits = []
    for t in after:
        if t is not None and queue.waited.get(id(t.sem), 0) < t.value:
            queue.waited[id(t.sem)] = t.value
            waits = [w for w in waits if w.sem is not t.sem] + [t]
    return waits


class Queue:

    def __init__(self, sem, latency):
        self.sem, self.latency, self.clock = sem, latency, 0.0
        self.count, self.items, self.waited, self.also = 0, [], {}, ()

    def do(self, make, after=(), signal=True, cost=0.1):
        after = [t for t in (*after, *self.also) if t is not None]
        self.also = ()
        self.clock = max([self.clock, *[t.time for t in after]]) + cost
        if signal:
            self.count += 1
        self.items.append((waits_of(self, after), make, signal))
        return Token(self.sem, self.count, self.clock + self.latency) if signal else None

    def mark(self):
        return Token(self.sem, self.count, self.clock)

    def replay(self, eng):
        for waits, make, signal in self.items:
            for t in waits:
                eng.wait_ge(t.sem, t.value)
            ins = make(eng)
            if signal:
                ins.then_inc(self.sem, 1)


class DmaQueue:

    def __init__(self, sems):
        self.sems, self.n, self.items, self.waited, self.clock = sems, 0, [], {}, 0.0

    def do(self, out, in_, after=()):
        after = [t for t in after if t is not None]
        self.clock = max([self.clock, *[t.time for t in after]]) + 0.45
        waits = waits_of(self, after)
        sem = self.sems[self.n % len(self.sems)]
        turn = self.n // len(self.sems)
        if turn and self.waited.get(id(sem), 0) < 16 * turn:
            waits.append(Token(sem, 16 * turn, 0.0))
            self.waited[id(sem)] = 16 * turn
        self.items.append((waits, out, in_, sem))
        self.n += 1
        return Token(sem, 16 * (turn + 1), self.clock + 2.0)

    def replay(self, eng):
        for waits, out, in_, sem in self.items:
            for t in waits:
                eng.wait_ge(t.sem, t.value)
            eng.dma_start(out, in_).then_inc(sem, 16)


def soonest(free):
    return min(range(len(free)), key=lambda i: max([t.time for t in free[i][1]], default=0.0))


class Slots:

    def __init__(self, items):
        self.free = [(x, ()) for x in items]

    def take(self, n=1):
        while len(self.free) < n:
            yield
        got = [self.free.pop(soonest(self.free)) for _ in range(n)]
        return got[0] if n == 1 else got

    def give(self, item, readers):
        self.free.append((item, tuple(t for t in readers if t is not None)))


class Banks:

    def __init__(self, psum):
        self.psum = psum
        self.free = [(i, ()) for i in range(8)]

    def take(self, beside=False):
        while not self.free:
            yield
        held = [i for i, _ in self.free]
        alone = [b for b in self.free if b[0] ^ 1 not in held] if beside else []
        if alone:
            got = alone[soonest(alone)]
            self.free.remove(got)
            return got
        return self.free.pop(soonest(self.free))

    def take_pair(self):
        while True:
            held = dict(self.free)
            for i, _ in self.free:
                j = i ^ 1
                if j in held:
                    a = min(i, j)
                    readers = tuple(held[i]) + tuple(held[j])
                    self.free = [x for x in self.free if x[0] not in (i, j)]
                    return a, readers
            yield

    def give(self, i, readers):
        self.free.append((i, tuple(readers)))

    def give_pair(self, i, readers):
        self.give(i, readers)
        self.give(i + 1, readers)


class Gate:

    def __init__(self, n):
        self.n = n

    def enter(self):
        while not self.n:
            yield
        self.n -= 1

    def leave(self):
        self.n += 1


def when(*marks):
    return max([t.time for t in marks if t is not None], default=0.0)


def step(queue, make, after=(), cost=0.1):
    yield when(*after)
    return queue.do(make, after, cost=cost)


def now(gen):
    while True:
        try:
            next(gen)
        except StopIteration as end:
            return end.value


class Task:
    live, now = [], 0.0

    def __init__(self, chain, name=None):
        self.chain, self.name, self.time, self.stuck, self.done = chain, name, Task.now, True, False
        Task.live.append(self)

    def go(self):
        try:
            said = next(self.chain)
        except StopIteration:
            self.done = True
            Task.live.remove(self)
            return True
        self.stuck = said is None
        if not self.stuck:
            self.time = said
        return not self.stuck


def together(chains, width=99):
    waiting, mine = list(chains), []
    while waiting or mine:
        mine = [t for t in mine if not t.done]
        while waiting and len(mine) < width:
            mine.append(Task(waiting.pop(0)))
        if mine:
            yield


def run_jobs(jobs, width):
    done, active, waiting = set(), [], list(jobs)
    while waiting or active:
        for job in list(waiting):
            if len(active) >= width:
                break
            if all(d in done for d in job[2]):
                waiting.remove(job)
                active.append(Task(job[1](), job[0]))
        before = list(Task.live)
        moved = any([t.go() for t in before if t.stuck]) or any(t not in before for t in Task.live)
        ready = [t for t in Task.live if not t.stuck]
        if ready and not moved:
            first = min(ready, key=lambda t: t.time)
            Task.now = max(Task.now, first.time)
            first.go()
        finished = {t.name for t in active if t.done}
        assert moved or ready or finished, ("no job can go on", [t.name for t in active])
        done |= finished
        active = [t for t in active if not t.done]


def build(nc, x_t, w0, w1, w2, w3, n0, n1, n2, n3, rw, cols, rows, mats, rope, zero, out):
    place = [nc.sbuf_base + 63 & ~63]

    def at(name, shape, dt, offset=None):
        size = 2 if dt == BF16 else 4
        for n in shape[1:]:
            size *= n
        where = place[0] if offset is None else offset
        if offset is None:
            place[0] = where + (size + 63 & ~63)
        return nc.alloc_sbuf_tensor_at(name, shape, dt, offset=where)

    NPAIR = 16
    X = at("x_res", [P, T], F32)
    colv = at("feature_cols", [P, NCOLS], F32)
    rowv = at("row_consts", [P, NROWS], F32)
    matf = at("const_mats", [P, KEPT_MATS], F32)
    matr = at("const_mats_r", [P, 2 * P], F32R)
    matb = at("const_mats_bf", [P, 3 * P], BF16)
    pickb = at("pick_bf", [96, 32], BF16)
    routerw = at("router_w", [P, NRW], F32)
    inv_width = at("inv_width", [P, 1], F32)
    minus_half = at("minus_half", [P, TPC], F32)
    euler = at("euler", [P, TPC * 9], F32)
    neg_a = at("neg_exp_alog", [P, 16], F32)
    s3half = at("half_w3s", [P, 1], F32)
    halves = at("halves", [P, 4], F32)
    tanh_cols = at("half_s1_and_half_s1_s2", [P, 8], F32)
    work = at("work_tiles", [P, 12, C], F32)
    pairs_t = at("pair_tiles", [P, NPAIR, 2, C], F32R)
    plain_t = at("pair_tiles_f32", [P, NPAIR, 2, C], F32, place[0] - NPAIR * 8 * C)
    small = at("small_tiles", [P, 6, 8], F32)
    smallr = at("small_tiles_r", [P, 6, 8], F32R)
    NS = 16
    w0n = at("attn0_weights", [P, N0_COLS], F32)
    region = place[0]
    w0r = at("ffn0_weights", [P, 2, L0W_COLS], F32R, region)
    attn_at = region + 8 * L0W_COLS
    NSTACK = 3
    qs_t = at("q_stacks", [P, NSTACK, 2, S], BF16, attn_at)
    ks_t = at("k_stacks", [P, NSTACK, 4, S], BF16, attn_at + 4 * NSTACK * S)
    v_at = attn_at + 12 * NSTACK * S
    v_t = at("v_rows", [P, 8, 176], F32, v_at)
    rope_t = at("rope", [P, 2, S], F32, v_at + 8 * 176 * 4)
    end_a = v_at + 8 * 176 * 4 + 8 * S
    w1r = at("moe1_weights", [P, 2, L1W_COLS], F32R, attn_at)
    w2r = at("moe2_weights", [P, 2, L2W_COLS], F32R, attn_at + 8 * L1W_COLS)
    w1n = at("mamba1_weights", [P, N1_COLS], F32, region)
    w2n = at("mamba2_weights", [P, N2_COLS], F32, region + 4 * N1_COLS)
    w3n = at("attn3_weights", [P, N3_COLS], F32, region + 4 * (N1_COLS + N2_COLS))
    free_b = region + 4 * (N1_COLS + N2_COLS + N3_COLS)
    EXTRA = 12
    extra = at("more_work_tiles", [P, EXTRA, C], F32, free_b)
    odds = free_b + EXTRA * 4 * C
    ones = at("ones", [P, P], F32, odds)
    tails = at("conv_tails", [P, NC_, 2, 4], F32, odds + 4 * P)
    states = at("scan_states", [P, NB, NS], F32, odds + 4 * P + 32 * NC_)
    NEXP = 5
    w3r = at("moe3_weights", [P, NEXP, 2, L3W_COLS], F32R, attn_at)
    EARLY = L1W_COLS // L3W_COLS
    assert max(end_a, free_b + EXTRA * 4 * C, attn_at + 8 * (L1W_COLS + L2W_COLS)) <= 229344, end_a
    assert odds + 4 * P + 32 * NC_ + 4 * NB * NS <= attn_at and NEXP * L3W_COLS <= L1W_COLS + L2W_COLS
    psum = nc.alloc_psum_tensor("banks", [P, 8, C], F32)

    gates_d = nc.dram_tensor("gates_d", [6 * NC_, 9 * C], F32, kind="Internal").ap()
    parts_d = nc.dram_tensor("parts_d", [NB, 2, 3, P, S], BF16, kind="Internal").ap()
    shift_d = nc.dram_tensor("shift_d", [NB, NH, 8, TILE], BF16, kind="Internal").ap()

    pe = Queue(nc.alloc_semaphore("pe_done"), 0.3)
    act = Queue(nc.alloc_semaphore("act_done"), 0.3)
    dve = Queue(nc.alloc_semaphore("dve_done"), 0.2)
    pool = Queue(nc.alloc_semaphore("pool_done"), 0.1)
    dma = DmaQueue([nc.alloc_semaphore(f"dma_done{i}") for i in range(32)])

    tiles = Slots([work[:, i, :] for i in range(12)])
    pair_views = [pairs_t[:, i, :, :] for i in range(NPAIR)]
    pairs = Slots(list(pair_views))
    smalls = Slots(list(range(6)))
    banks = Banks(psum)

    def plain(pair):
        return plain_t[:, [v is pair for v in pair_views].index(True), :, :]

    def col(name, i=0):
        return colv[:, COLS[name] + i:COLS[name] + i + 1]

    ident = matf[:, 0:P]
    heads = matf[:, MATS["heads"]:MATS["heads"] + P]
    ident_r, centre_r = matr[:, 0:P], matr[:, P:2 * P]
    ident_b, mask_st, mask_ts = matb[:, 0:P], matb[:, P:2 * P], matb[:, 2 * P:3 * P]

    def size(o):
        n = 1
        for k in o.shape[1:]:
            n *= k
        return n

    def on_act(make, o, after):
        return step(act, make, after, 0.11 + size(o) / 1200)

    def on_dve(make, o, after, rate=0.96):
        return step(dve, make, after, 0.08 + size(o) / 1000 / rate)

    def copy_act(o, i, after):
        return on_act(lambda e: e.activation(o, i, ACT.Copy), o, after)

    def func(f, o, i, after, **kw):
        return on_act(lambda e: e.activation(o, i, f, **kw), o, after)

    def copy_dve(o, i, after):
        return on_dve(lambda e: e.tensor_copy(o, i), o, after)

    def tt(o, a, b, op, after, q=None):
        if q is pool:
            return step(pool, lambda e: e.tensor_tensor(o, a, b, op), after, 1.2 + size(o) / 2000)
        return on_dve(lambda e: e.tensor_tensor(o, a, b, op), o, after)

    def ts(o, a, s1, op0, after, s2=None, op1=None):
        if op1 is None:
            return on_dve(lambda e: e.tensor_scalar(o, a, s1, None, op0), o, after)
        return on_dve(lambda e: e.tensor_scalar(o, a, s1, s2, op0, op1), o, after)

    def stt(o, a, s, b, op0, op1, after):
        return on_dve(lambda e: e.scalar_tensor_tensor(out=o, in0=a, scalar=s, in1=b, op0=op0, op1=op1), o, after)

    def reciprocal(o, a, after):
        return step(dve, lambda e: e.reciprocal(o, a), after, 0.1 + size(o) / 155)

    def mm(o, l, r, start, stop, after=(), signal=False):
        passes = 4 if r.dtype == F32 else 1
        return pe.do(lambda e: e.matmul(o, l, r, start=start, stop=stop), after, signal,
                     max(size(r) * passes / 2400, 0.03))

    def split(src, pair, after, free):
        hi = yield from copy_act(pair[:, 0, :], src, [*after, *free])
        lo = yield from tt(pair[:, 1, :], src, pair[:, 0, :].bitcast(F32), ALU.subtract, [hi, *after])
        return [hi, lo]

    def split_mm(o, terms, after):
        n = len(terms)
        yield when(*after, *[m for t in terms for m in t[3]])
        for i, (wh, wl, pair, marks) in enumerate(terms):
            mm(o, wh, pair[:, 0, :], i == 0, False, [*after, marks[0]])
            mm(o, wl, pair[:, 0, :], False, False)
            done = mm(o, wh, pair[:, 1, :], False, i == n - 1, [marks[1]], i == n - 1)
        return done

    def product(o, w, x, after):
        yield when(*after)
        return mm(o, w, x, True, True, after, True)

    def full_mm(o, terms, after):
        n = len(terms)
        yield when(*after, *[m for t in terms for m in t[2]])
        for i, (w, x, marks) in enumerate(terms):
            done = mm(o, w, x, i == 0, i == n - 1, [*after, *marks], i == n - 1)
        return done

    stage, sfree = None, ()
    d_cols = dma.do(colv[:, :], cols)
    d_rows = dma.do(rowv[:, :], rows)
    d_mats = dma.do(matf[:, :], mats[:, 0:KEPT_MATS])
    raw = work[:, 0, :]
    d_raw = dma.do(raw[:, 0:NMATS - KEPT_MATS], mats[:, KEPT_MATS:NMATS])
    d_rw = dma.do(routerw[:, :], rw)
    x_ready = [[dma.do(X[:, c * C:(c + 1) * C], x_t[:, c * C:(c + 1) * C])] for c in range(NC_)]
    c_ready = [now(copy_dve(ident_r, ident, [d_mats])), now(copy_dve(centre_r, raw[:, 0:P], [d_raw])),
               now(copy_dve(ident_b, ident, [d_mats])), now(copy_dve(matb[:, P:3 * P], raw[:, P:3 * P], [d_raw]))]
    c_ready.append(now(copy_dve(pickb[:, :], raw[0:96, 3 * P:3 * P + 32], [d_raw])))
    for tile, value in ((inv_width, 1.0 / P), (minus_half, -0.5), (halves, 0.5), (euler, EULER)):
        c_ready.append(dve.do(lambda e, tile=tile, value=value: e.memset(tile[:, :], value)))
    c_ready.append(now(ts(s3half[:, :], col("w3s"), 0.5, ALU.mult, [d_cols])))
    c_ready.append(now(tt(tanh_cols[:, 0:4], colv[:, COLS["s1"]:COLS["s1"] + 4], halves[:, :], ALU.mult, [c_ready[-1]])))
    c_ready.append(now(tt(tanh_cols[:, 4:8], tanh_cols[:, 0:4], colv[:, COLS["s2"]:COLS["s2"] + 4], ALU.mult,
                          [c_ready[-1]])))
    for q in (pe, act, dve, pool):
        q.also = [c_ready[-1], d_cols, d_rows, d_mats, d_rw]
    tiles.free[0] = (tiles.free[0][0], (c_ready[-1],))

    def load_native(dst, src, after):
        return dma.do(dst[:, :], src, after)

    def load_split(dst, src, ncols, after, marks):
        for c0 in range(0, ncols, C):
            n = min(C, ncols - c0)
            t, tf = yield from tiles.take()
            yield when(*tf, *after)
            d = dma.do(t[:, 0:n], src[:, c0:c0 + n], [*tf, *after])
            hi = yield from copy_dve(dst[:, 0, c0:c0 + n], t[:, 0:n], [d, *after])
            lo = yield from tt(dst[:, 1, c0:c0 + n], t[:, 0:n], dst[:, 0, c0:c0 + n].bitcast(F32), ALU.subtract, [hi])
            tiles.give(t, [hi, lo])
            marks.append(lo)

    def layernorm(src, after, gain=None, bias=None):
        yield when(*after)
        pair, pf = yield from pairs.take()
        xs = yield from split(src, pair, after, pf)
        b, bf = yield from banks.take()
        pc = psum[:, b, :]
        yield when(*xs, *bf)
        mm(pc, centre_r, pair[:, 0, :], True, False, [xs[0], *bf])
        centred = mm(pc, centre_r, pair[:, 1, :], False, True, [xs[1]], True)
        pairs.give(pair, [centred])
        (sq, f1), (xc, f2) = yield from tiles.take(2)
        squared = yield from func(ACT.Square, sq, pc, [centred, *f1])
        copied = yield from copy_act(xc, pc, [centred, *f2])
        banks.give(b, [copied])
        b, bf = yield from banks.take()
        yield when(squared, *bf)
        for t in range(TPC):
            var = mm(psum[:, b, t:t + 1], sq[:, t * TILE:(t + 1) * TILE], inv_width[:, :], True, True,
                     [squared, *bf], t == TPC - 1)
        tiles.give(sq, [var])
        k, kf = yield from smalls.take()
        s, r = small[:, k, :], smallr[:, k, :]
        veps = yield from ts(s[:, 0:4], psum[:, b, 0:4], EPS, ALU.add, [var, *kf])
        rstd = yield from tt(s[:, 4:8], s[:, 0:4], minus_half[:, :], ALU.pow, [veps], pool)
        rhi = yield from copy_dve(r[:, 0:4], s[:, 4:8], [rstd])
        rlo = yield from tt(r[:, 4:8], s[:, 4:8], r[:, 0:4].bitcast(F32), ALU.subtract, [rhi])
        yield when(rlo)
        for t in range(TPC):
            for part in (0, 4):
                spread = mm(psum[:, b, t * TILE:(t + 1) * TILE], r[:, part + t:part + t + 1].broadcast_to([P, P]),
                            ident_r, part == 0, part == 4, [rlo], t == TPC - 1 and part == 4)
        smalls.give(k, [spread])
        done = yield from tt(xc, psum[:, b, :], xc, ALU.mult, [spread, copied])
        banks.give(b, [done])
        if gain is not None:
            done = yield from ts(xc, xc, gain, ALU.mult, [done], bias, ALU.add)
        return xc, [done]

    def hidden(f, terms, after, slot, **kw):
        p, pf = slot
        h, hf = yield from tiles.take()
        b, bf = yield from banks.take()
        z = yield from split_mm(psum[:, b, :], terms, [*bf, *after])
        hi = yield from func(f, p[:, 0, :], psum[:, b, :], [z, *pf], **kw)
        a = yield from func(f, h, psum[:, b, :], [z, *hf], **kw)
        banks.give(b, [a])
        lo = yield from tt(p[:, 1, :], h, p[:, 0, :].bitcast(F32), ALU.subtract, [a, hi])
        tiles.give(h, [lo])
        return [hi, lo], z

    w0_marks, ffn_done = [], []
    gate0 = Gate(2)

    def w0_parts(name, i):
        c0 = L0W[name] + i * P
        return w0r[:, 0, c0:c0 + P], w0r[:, 1, c0:c0 + P]

    def ffn0(c):
        xs = X[:, c * C:(c + 1) * C]
        xn, xm = yield from layernorm(xs, x_ready[c])
        yield from gate0.enter()
        xp, pf = yield from pairs.take()
        marks = yield from split(xn, xp, xm, pf)
        tiles.give(xn, marks)
        while len(w0_marks) < 2:
            yield
        hid = yield from pairs.take(4)
        hid_m, zs = [None] * 4, []

        def gated(f):
            h, hf = yield from tiles.take()
            b1, bf = yield from banks.take()
            up = yield from split_mm(psum[:, b1, :], [(*w0_parts("w1", f), xp, marks)], [*bf, w0_marks[0]])
            a = yield from func(ACT.Tanh, h, psum[:, b1, :], [up, *hf], scale=tanh_cols[:, f:f + 1])
            a = yield from stt(h, h, 1.0, psum[:, b1, :], ALU.add, ALU.mult, [a])
            banks.give(b1, [a])
            b2, bf = yield from banks.take()
            gt = yield from split_mm(psum[:, b2, :], [(*w0_parts("w2", f), xp, marks)], [*bf, w0_marks[1]])
            g = yield from stt(h, psum[:, b2, :], tanh_cols[:, 4 + f:5 + f], h, ALU.mult, ALU.mult, [gt, a])
            banks.give(b2, [g])
            p, pf = hid[f]
            hid_m[f] = yield from split(h, p, [g], pf)
            tiles.give(h, hid_m[f])
            zs.append(gt)

        yield from together([gated(f) for f in range(4)])
        pairs.give(xp, zs)
        for name, scale in (("h1", "h1s"), ("h2", "h2s")):
            while len(w0_marks) <= (L0W[name] + 2047) // C:
                yield
            nxt = yield from pairs.take(4)
            nxt_m, zs = [None] * 4, []

            def layer(o):
                wide = [(*w0_parts(name, 4 * k + o), hid[k][0], hid_m[k]) for k in range(4)]
                nxt_m[o], z = yield from hidden(ACT.Gelu, wide, [w0_marks[(L0W[name] + 2047) // C]], nxt[o],
                                                scale=col(scale, o))
                zs.append(z)

            yield from together([layer(o) for o in range(4)])
            for p, _ in hid:
                pairs.give(p, zs)
            hid, hid_m = nxt, nxt_m
        b, bf = yield from banks.take()
        z = yield from split_mm(psum[:, b, :], [(*w0_parts("w3", k), hid[k][0], hid_m[k]) for k in range(4)],
                                [*bf, w0_marks[-1]])
        for p, _ in hid:
            pairs.give(p, [z])
        gate0.leave()
        done = yield from stt(xs, psum[:, b, :], s3half[:, :], xs, ALU.mult, ALU.add, [z])
        banks.give(b, [done])
        x_ready[c] = [done]
        ffn_done.append(c)

    Q_PART = (0, 0, 1, 0, 2, 1)
    K_PART = (0, 1, 0, 2, 0, 1)
    ROWS_H = 6 * HD
    stack_slots = Slots(list(range(NSTACK)))
    stack_marks = {"readers": ()}
    k_ones, weighing = [], [-1]
    AHEAD = 1

    def attn_setup():
        t, tf = yield from tiles.take()
        ones_b = t.bitcast(BF16)
        one = yield from step(dve, lambda e: e.memset(ones_b, 1.0), tf)
        cleared = yield from step(dve, lambda e: e.memset(ks_t.bitcast(F32)[:, :, :, :], 0.0))
        cleared = yield from step(dve, lambda e: e.memset(qs_t.bitcast(F32)[:, :, :, :], 0.0))
        d = [dma.do(ks_t[64 * h + ROWS_H:64 * h + ROWS_H + 1, n, h:4:2, :], ones_b[0:2, :], [one, cleared])
             for h in range(2) for n in range(NSTACK)]
        tiles.give(t, d)
        k_ones.extend(d)
        k_ones.append((yield from step(dve, lambda e: e.memset(v_t[:, :, :], 1.0))))
        k_ones.append(dma.do(rope_t[:, :, :], rope))
        k_ones.append(load_native(w0n, n0, []))

    def project_heads(b, half, written):
        c = 2 * b + half
        xn, xm = yield from layernorm(X[:, c * C:(c + 1) * C], x_ready[c])
        where = slice(half * C, half * C + C)
        for side_, (w, ws, bias, bias_s) in enumerate((("q", "qs", "bq", "bqs"), ("k", "ks", "bk", "bks"))):
            turned = []
            for name, bn, table in ((w, bias, 0), (ws, bias_s, 1)):
                bk, bf = yield from banks.take()
                z = yield from full_mm(psum[:, bk, :], [(w0n[:, N0[name]:N0[name] + P], xn, [*xm, *k_ones])], bf)
                t, tf = yield from tiles.take()
                r = yield from stt(t, psum[:, bk, :], col(bn), rope_t[:, table, where], ALU.add, ALU.mult, [z, *tf, *k_ones])
                banks.give(bk, [r])
                turned.append((t, r))
            (t0, r0), (t1, r1) = turned
            full = yield from tt(t0, t0, t1, ALU.add, [r0, r1])
            (p01, f01), (p2, f2) = yield from tiles.take(2)
            hi, mid = p01.bitcast(BF16)[:, 0:C], p01.bitcast(BF16)[:, C:2 * C]
            lo = p2.bitcast(BF16)[:, 0:C]
            m0 = yield from copy_act(hi, t0, [full, *f01])
            rest = yield from tt(t1, t0, hi, ALU.subtract, [m0])
            m1 = yield from copy_act(mid, t1, [rest])
            m2 = yield from tt(lo, t1, mid, ALU.subtract, [m1, *f2])
            tiles.give(t0, [m0, rest])
            tiles.give(t1, [m1, m2])
            yield when(m2)
            d = [dma.do(parts_d[b, side_, 0, :, where], hi, [m0]), dma.do(parts_d[b, side_, 1, :, where], mid, [m1]),
                 dma.do(parts_d[b, side_, 2, :, where], lo, [m2])]
            tiles.give(p01, [m2, *d[0:2]])
            tiles.give(p2, [d[2]])
            written.extend(d)
        return xn, xm

    def project_v(b, half, xn, xm, written):
        bk, bf = yield from banks.take()
        yield when(*xm, *bf)
        for t in range(TPC):
            z = mm(psum[:, bk, t * TILE:(t + 1) * TILE], xn[:, t * TILE:(t + 1) * TILE],
                   w0n[:, N0["v"]:N0["v"] + P], True, True, [*xm, *bf], t == TPC - 1)
        tiles.give(xn, [z])
        rows_v = v_t[:, half * TPC:(half + 1) * TPC, 0:NH * 9].rearrange("p t (h c) -> p t h c", c=9)
        for t in range(TPC):
            v = yield from tt(rows_v[:, t, :, 0:HD], psum[:, bk, t * TILE:(t + 1) * TILE].rearrange("p (h c) -> p h c", c=HD),
                   rowv[:, ROWS["bv"]:ROWS["bv"] + P].rearrange("p (h c) -> p h c", c=HD), ALU.add,
                   [z, *stack_marks["readers"], *k_ones])
        banks.give(bk, [v])
        written.append(v)

    gate_a = Gate(2)

    def attn_gate_v(b):
        while stack_marks.get("done", -1) < b - 1:
            yield

    def attention(b):
        yield from gate_a.enter()
        written, v_ready, stacks = [], [], {}

        normed = []
        for half in range(2):
            normed.append((half, *(yield from project_heads(b, half, written))))

        def load_stacks(g):
            k_, free = yield from stack_slots.take()
            yield when(*written, *free, *k_ones)
            marks = []
            for h in range(2):
                for side_, order in ((0, Q_PART), (1, K_PART)):
                    for s_, part in enumerate(order):
                        at_ = 64 * h + HD * s_
                        src = parts_d[b, side_, part].rearrange("(j h d) t -> h d j t", h=2, d=HD)[h, :, 2 * g:2 * g + 2]
                        dst = qs_t[at_:at_ + HD, k_, :, :] if side_ == 0 else ks_t[at_:at_ + HD, k_, h:4:2, :]
                        marks.append(dma.do(dst, src, [*written, *free, *k_ones]))
                marks.append(dma.do(qs_t[64 * h + ROWS_H:64 * h + ROWS_H + 1, k_, :, :],
                                    zero.bitcast(BF16).rearrange("p (j t) -> p j t", j=2), [*free, *k_ones]))
            stacks[g] = (k_, marks)

        shifts = {}

        def q_of(h, j0, j1):
            return qs_t[:, stacks[h // 4][0], h % 4 // 2, j0:j1]

        def k_of(h, j0, j1):
            return ks_t[:, stacks[h // 4][0], h % 4, j0:j1]

        def find_max(g):
            while g not in stacks or weighing[0] < 4 * b + g - AHEAD:
                yield
            mx, mf = yield from tiles.take()
            best = mx[:, 0:32].rearrange("p (h i) -> p h i", h=4)
            marks = []

            def search(i, h0, per):
                wide = (i + 1) * TILE
                bk, bf = yield from banks.take_pair()
                both = psum[:, bk:bk + 2, :].rearrange("p a c -> p (a c)")
                pitch = wide if per == 4 else C if per == 2 else 0
                yield when(*bf, *stacks[g][1])
                for n in range(per):
                    h = 4 * g + h0 + n
                    for k0 in range(0, wide, C):
                        k1 = min(k0 + C, wide)
                        diag = k1 == wide
                        z = mm(both[:, n * pitch + k0:n * pitch + k1],
                               q_of(h, i * TILE, (i + 1) * TILE), k_of(h, k0, k1),
                               True, not diag, [*bf, *stacks[g][1]], False)
                        if diag:
                            z = mm(both[:, n * pitch + k1 - TILE:n * pitch + k1], ident_b, mask_st, False, True,
                                   [], True)
                view = psum[:, bk:bk + 2, 0:wide] if per == 2 else \
                    both[:, 0:per * wide].rearrange("p (n c) -> p n c", n=per)
                m = yield from step(dve, lambda e: e.tensor_reduce(best[:, h0:h0 + per, i], view, AX.X, ALU.max),
                                    [z, *mf], 0.1 + per * wide / 960)
                banks.give_pair(bk, [m])
                marks[:] = [m]

            per_of = [4, 4, 2, 2, 1, 1, 1, 1]
            yield from together([search(i, h0, per_of[i]) for i in range(8) for h0 in range(0, 4, per_of[i])], 2)
            bk, bf = yield from banks.take()
            yield when(*marks, *bf)
            z = yield from product(psum[0:32, bk, 0:TILE], mx[:, 0:32], ident, [*marks, *bf])
            low = mx[0:32, 64:128].bitcast(BF16)
            n = yield from ts(low, psum[0:32, bk, 0:TILE], -1.0, ALU.mult, [z])
            banks.give(bk, [n])
            yield when(n)
            d = dma.do(shift_d[b, 4 * g:4 * g + 4].rearrange("h i s -> (h i) s"), low, [n])
            tiles.give(mx, [d])
            yield when(d)
            shifts[g] = [dma.do(qs_t[64 * h + ROWS_H:64 * h + ROWS_H + 1, stacks[g][0], :, :],
                                shift_d[b, 4 * g:4 * g + 4].rearrange("(j h) i s -> h j (i s)", h=2)[h:h + 1],
                                [d]) for h in range(2)]

        taken = []
        found = []

        def weigh(g):
            while g not in shifts:
                yield
            weighing[0] = 4 * b + g
            both_halves, hf = yield from pairs.take()
            for half in range(2):
                acc, af = yield from banks.take(beside=True)
                last = TPC * (half + 1)
                weights, y = {}, []

                def score(i, pr):
                    slot, pf = yield from pairs.take()
                    q0 = max(0, i * TILE - half * C)
                    n = C - q0
                    diag = i >= TPC * half
                    weighted = []

                    def head(n_):
                        bk, bf = yield from banks.take(beside=True)
                        yield when(*bf, *shifts[g])
                        h = 4 * g + 2 * pr + n_
                        z = mm(psum[:, bk, 0:n], k_of(h, i * TILE, (i + 1) * TILE),
                               q_of(h, half * C + q0, half * C + C), True, not diag, [*bf, *shifts[g]], not diag)
                        if diag:
                            z = mm(psum[:, bk, 0:TILE], ident_b, mask_ts, False, True, [], True)
                        x = yield from func(ACT.Exp, plain(slot)[:, n_, 0:n], psum[:, bk, 0:n], [z, *pf],
                                            scale=HD ** -0.5)
                        banks.give(bk, [x])
                        weighted.append(x)

                    yield from together([head(0), head(1)])
                    weights[i, pr] = (slot, weighted, q0, n)

                def scores():
                    yield from together([score(i, pr) for i in range(last) for pr in range(2)], 2)

                def add_rows():
                    for i in range(last):
                        while (i, 0) not in weights or (i, 1) not in weights:
                            yield
                        yield when(*weights[i, 0][1], *weights[i, 1][1], *af, *v_ready)
                        for k in range(4):
                            slot, marks, q0, n = weights[i, k // 2]
                            c9 = 9 * (4 * g + k)
                            y[:] = [pe.do(lambda e, o=psum[32 * k:32 * k + 32, acc, q0:C], l=v_t[:, i, c9:c9 + 32],
                                          r=plain(slot)[:, k % 2, 0:n], st=(i == 0), en=(i == last - 1), k=k:
                                          e.matmul(o, l, r, start=st, stop=en, tile_position=(0, 32 * k)),
                                          [*marks, *af, *v_ready], cost=n / 2400)]
                        for pr in range(2):
                            pairs.give(weights[i, pr][0], y)

                yield from together([add_rows(), scores()])
                t = plain(both_halves)[:, half, :]
                m = yield from copy_dve(t, psum[:, acc, :], [*y, *hf])
                banks.give(acc, [m])
                found.append((g, half, t, m))
                if half:
                    stack_slots.give(stacks[g][0], [pe.mark()])
            taken.append(both_halves)

        def finish(half):
            mine = [f for f in found if f[1] == half]
            o, of = yield from tiles.take()
            bn, fn = yield from banks.take()
            bd, fd = yield from banks.take()
            yield when(*fn, *fd, *[f[3] for f in mine])
            for name, bank, free in (("num", bn, fn), ("den", bd, fd)):
                for n_, (g, _, t, m) in enumerate(mine):
                    c0 = MATS[name] + 96 - 32 * g
                    z = mm(psum[:, bank, :], matf[:, c0:c0 + P], t, n_ == 0, n_ == 3, [m, *free], n_ == 3)
            r = yield from reciprocal(o, psum[:, bd, :], [z, *of])
            a = yield from tt(o, psum[:, bn, :], o, ALU.mult, [r])
            banks.give(bn, [a])
            z2 = yield from full_mm(psum[:, bd, :], [(w0n[:, N0["o"]:N0["o"] + P], o, [a])], [r])
            tiles.give(o, [z2])
            c = 2 * b + half
            xs = X[:, c * C:(c + 1) * C]
            done = yield from stt(xs, psum[:, bd, :], col("bo"), xs, ALU.add, ALU.add, [z2])
            banks.give(bd, [done])
            x_ready[c] = [done]
            return z

        def find_all():
            while stack_marks.get("found", -1) < b - 1:
                yield
            def load_all():
                for g in range(4):
                    yield from load_stacks(g)

            def search_all():
                for g in range(4):
                    yield from find_max(g)

            yield from together([load_all(), search_all()])
            stack_marks["found"] = b

        def weigh_all():
            yield from attn_gate_v(b)
            rows = []
            for half, xn, xm in normed:
                yield from project_v(b, half, xn, xm, rows)
            v_ready.extend(rows)
            while len(ffn_done) < NC_:
                yield
            for g in range(4):
                yield from weigh(g)
            stack_marks["readers"] = (pe.mark(),)
            stack_marks["done"] = b
            for half in range(2):
                z = yield from finish(half)
            for p in taken:
                pairs.give(p, [z])
            gate_a.leave()

        yield from together([find_all(), weigh_all()])

    def every(v):
        return v.unsqueeze(2).broadcast_to([P, TPC, E8])

    def gates(number, kind, xn, xm):
        ne = 9 if kind == "l2" else 8
        b, bf = yield from banks.take()
        yield when(*xm, *bf)
        for t in range(TPC):
            z = mm(psum[:, b, t * ne:(t + 1) * ne], xn[:, t * TILE:(t + 1) * TILE],
                   routerw[:, RW[kind]:RW[kind] + ne], True, True, [*xm, *bf], t == TPC - 1)
        (r, rf), (o, of) = yield from tiles.take(2)
        logits = psum[:, b, 0:TPC * ne].rearrange("p (t e) -> p t e", e=ne)

        def grid(k):
            return r[:, 32 * k:32 * k + 32].rearrange("p (t e) -> p t e", e=E8)

        def line(k):
            return r[:, 480 + 4 * k:484 + 4 * k]

        def row(name):
            return rowv[:, ROWS[name]:ROWS[name] + E8].unsqueeze(1).broadcast_to([P, TPC, E8])

        def best(v, o_, after):
            return (yield from step(dve, lambda e: e.tensor_reduce(o_, v, AX.X, ALU.max), after))

        power = euler[:, 0:32].rearrange("p (t e) -> p t e", e=E8)
        lg = grid(0)
        if kind == "l2":
            m = yield from copy_dve(lg, logits[:, :, 0:E8], [z, *rf])
            m9 = yield from ts(line(6), logits[:, :, 8], -1.0, ALU.mult, [m])
        else:
            m = yield from tt(lg, logits, row("br1" if kind == "l1" else "br3"), ALU.add, [z, *rf])
        banks.give(b, [dve.mark()])
        if kind != "l3":
            m = yield from best(lg, line(0), [m])
            m = yield from tt(grid(1), lg, every(line(0)), ALU.subtract, [m])
            m = yield from step(pool, lambda e: e.tensor_tensor(grid(1), power, grid(1), ALU.pow), [m], 1.25)
            m = yield from step(dve, lambda e: e.tensor_reduce(line(1), grid(1), AX.X, ALU.add), [m])
            m = yield from step(dve, lambda e: e.reciprocal(line(1), line(1)), [m])
            m = yield from tt(lg, grid(1), every(line(1)), ALU.mult, [m])
        for k, at_ in ((0, 2), (1, 6)):
            src = lg if k == 0 else grid(10)
            top, code, first, mark_ = line(2 + k), grid(at_), line(4), grid(at_ + 1)
            m = yield from best(src, top, [m])
            m = yield from tt(code, src, every(top), ALU.is_equal, [m])
            m = yield from tt(code, code, row("code"), ALU.mult, [m])
            m = yield from best(code, first, [m])
            m = yield from tt(mark_, code, every(first), ALU.is_equal, [m])
            if k == 0:
                m = yield from stt(grid(10), mark_, NEG, lg, ALU.mult, ALU.add, [m])
        one, two = grid(3), grid(7)
        gate = o[:, 0:TPC * ne].rearrange("p (e t) -> p t e", t=TPC)
        if kind == "l1":
            m = yield from stt(one, one, 0.5, lg[:, :, 0:1].broadcast_to([P, TPC, E8]), ALU.mult, ALU.mult, [m])
            m = yield from stt(two, two, 0.5, lg[:, :, 1:2].broadcast_to([P, TPC, E8]), ALU.mult, ALU.mult, [m])
            m = yield from tt(gate, one, two, ALU.add, [m, *of])
        elif kind == "l2":
            m = yield from tt(one, one, two, ALU.add, [m])
            m = yield from stt(gate[:, :, 0:E8], one, 0.5, lg, ALU.mult, ALU.mult, [m, *of])
            m = yield from step(pool, lambda e: e.tensor_tensor(line(6), euler[:, 0:TPC], line(6), ALU.pow), [m, m9], 1.25)
            m = yield from ts(line(6), line(6), 1.0, ALU.add, [m], 2.0, ALU.mult)
            m = yield from step(dve, lambda e: e.reciprocal(gate[:, :, 8], line(6)), [m])
        else:
            m = yield from tt(line(5), line(3), line(2), ALU.subtract, [m])
            m = yield from step(pool, lambda e: e.tensor_tensor(line(5), euler[:, 0:TPC], line(5), ALU.pow), [m], 1.25)
            m = yield from ts(line(6), line(5), 1.0, ALU.add, [m])
            m = yield from step(dve, lambda e: e.reciprocal(line(6), line(6)), [m])
            m = yield from tt(line(5), line(5), line(6), ALU.mult, [m])
            m = yield from tt(one, one, every(line(6)), ALU.mult, [m])
            m = yield from tt(two, two, every(line(5)), ALU.mult, [m])
            m = yield from tt(gate, one, two, ALU.add, [m, *of])
        b, bf = yield from banks.take()
        z = yield from product(psum[0:TPC * ne, b, 0:TILE], o[:, 0:TPC * ne], ident, [m, *bf])
        tiles.give(r, [m])
        m = yield from copy_dve(o[0:TPC * ne, 128:128 + TILE], psum[0:TPC * ne, b, 0:TILE], [z])
        banks.give(b, [m])
        yield when(m)
        d = dma.do(gates_d[number, 0:ne * C].rearrange("(r k) -> r k", k=TILE), o[0:TPC * ne, 128:128 + TILE], [m])
        tiles.give(o, [d])
        return d

    def gate_tile(number, e, written):
        t, tf = yield from tiles.take()
        yield when(written, *tf)
        d = dma.do(t, gates_d[number:number + 1, e * C:(e + 1) * C].broadcast_to([P, C]), [written, *tf])
        return t, d

    def weighed(target, marks, bank, y, gate, bias=None):
        t, d = gate
        if bias is None:
            m = yield from tt(t, psum[:, bank, :], t, ALU.mult, [y, d])
        else:
            m = yield from stt(t, psum[:, bank, :], bias, t, ALU.add, ALU.mult, [y, d])
        banks.give(bank, [m])
        yield when(m)
        marks[:] = [pool.do(lambda e: e.tensor_tensor(target, target, t, ALU.add), [m, *marks], cost=1.45)]
        tiles.give(t, marks)

    gate_moe, front = Gate(2), Gate(3)
    WIDE = 5
    w1_marks, w2_marks = [], []

    def parts(w, c0):
        return w[:, 0, c0:c0 + P], w[:, 1, c0:c0 + P]

    def moe1(c, number):
        xs = X[:, c * C:(c + 1) * C]
        yield from front.enter()
        xn, xm = yield from layernorm(xs, x_ready[c])
        written = yield from gates(number, "l1", xn, xm)
        yield from gate_moe.enter()
        front.leave()
        xp, pf = yield from pairs.take()
        marks = yield from split(xn, xp, xm, pf)
        tiles.give(xn, marks)
        while len(w1_marks) < L1W_COLS // C:
            yield
        zs = []

        def expert(e):
            p, pf = yield from pairs.take()
            m, z = yield from hidden(ACT.Relu, [(*parts(w1r, 3 * e * P), xp, marks)], [w1_marks[-1]], (p, pf),
                                     bias=col("l1b1", e))
            zs.append(z)
            m, z = yield from hidden(ACT.Relu, [(*parts(w1r, (3 * e + 1) * P), p, m)], [], (p, []),
                                     bias=col("l1b2", e))
            gate = yield from gate_tile(number, e, written)
            b, bf = yield from banks.take()
            z = yield from split_mm(psum[:, b, :], [(*parts(w1r, (3 * e + 2) * P), p, m)], bf)
            pairs.give(p, [z])
            yield from weighed(xs, x_ready[c], b, z, gate, col("l1b3", e))

        yield from together([expert(e) for e in range(E8)], WIDE)
        pairs.give(xp, zs)
        gate_moe.leave()

    def moe2(c, number):
        xs = X[:, c * C:(c + 1) * C]
        yield from front.enter()
        xn, xm = yield from layernorm(xs, x_ready[c])
        written = yield from gates(number, "l2", xn, xm)
        yield from gate_moe.enter()
        front.leave()
        xp, pf = yield from pairs.take()
        marks = yield from split(xn, xp, xm, pf)
        tiles.give(xn, marks)
        while len(w2_marks) < -(-L2W_COLS // C):
            yield
        zs = []

        def expert(e):
            p, pf = yield from pairs.take()
            if e < E8:
                m, z = yield from hidden(ACT.Silu, [(*parts(w2r, 2 * e * P), xp, marks)], [w2_marks[-1]], (p, pf))
            else:
                h, hf = yield from tiles.take()
                b1, bf = yield from banks.take()
                z = yield from split_mm(psum[:, b1, :], [(*parts(w2r, L2W_GU), xp, marks)], [w2_marks[-1], *bf])
                a = yield from func(ACT.Silu, h, psum[:, b1, :], [z, *hf])
                banks.give(b1, [a])
                b2, bf = yield from banks.take()
                z = yield from split_mm(psum[:, b2, :], [(*parts(w2r, L2W_GU + P), xp, marks)], bf)
                a = yield from tt(h, psum[:, b2, :], h, ALU.mult, [z, a])
                banks.give(b2, [a])
                m = yield from split(h, p, [a], pf)
                tiles.give(h, m)
            zs.append(z)
            gate = yield from gate_tile(number, e, written)
            b, bf = yield from banks.take()
            w = (2 * e + 1) * P if e < E8 else L2W_DOWN
            z = yield from split_mm(psum[:, b, :], [(*parts(w2r, w), p, m)], bf)
            pairs.give(p, [z])
            yield from weighed(xs, x_ready[c], b, z, gate)

        yield from together([expert(e) for e in range(9)], WIDE)
        pairs.give(xp, zs)
        gate_moe.leave()

    slots3 = Slots([])
    front3 = Gate(1)
    loaded3, users3, entered3 = {}, {}, {}

    def stream3(number):
        for u in range(NC_ // 2):
            for e in range(E8):
                k, kf = yield from slots3.take()
                marks = []
                yield from load_split(w3r[:, k, :, :], w3[e], L3W_COLS, kf, marks)
                loaded3[number, u, e] = (k, marks)

    def moe3(c, number):
        xs = X[:, c * C:(c + 1) * C]
        fronted, entered = entered3.setdefault(number // NC_, (set(), set()))
        while c and c - 1 not in fronted:
            yield
        yield from front3.enter()
        fronted.add(c)
        xn, xm = yield from layernorm(xs, x_ready[c])
        written = yield from gates(number, "l3", xn, xm)
        while c and c - 1 not in entered:
            yield
        yield from gate_moe.enter()
        entered.add(c)
        front3.leave()
        xp, pf = yield from pairs.take()
        marks = yield from split(xn, xp, xm, pf)
        total = [*xm, *marks]
        zs = []

        def expert(e):
            key = (number // NC_, c // 2, e)
            while key not in loaded3:
                yield
            k, wm = loaded3[key]
            gate = yield from gate_tile(number, e, written)
            b, bf = yield from banks.take()
            added = []

            def block(f):
                p, pf = yield from pairs.take()
                m, z = yield from hidden(ACT.Relu, [(*parts(w3r[:, k, :, :], f * P), xp, marks)], wm, (p, pf),
                                         bias=col("l3b1", 4 * e + f))
                zs.append(z)
                yield when(*m, *bf)
                wh, wl = parts(w3r[:, k, :, :], (4 + f) * P)
                mm(psum[:, b, :], wh, p[:, 0, :], not added, False, [m[0], *bf])
                mm(psum[:, b, :], wl, p[:, 0, :], False, False)
                added.append(mm(psum[:, b, :], wh, p[:, 1, :], False, len(added) == 3, [m[1]], True))
                pairs.give(p, [added[-1]])

            yield from together([block(f) for f in range(4)], 3)
            users3[key] = users3.get(key, ()) + (added[-1],)
            if len(users3[key]) == 2:
                slots3.give(k, users3[key])
            yield from weighed(xn, total, b, added[-1], gate, col("l3b2", e))

        yield from together([expert(e) for e in range(E8)], 2)
        pairs.give(xp, zs)
        gate_moe.leave()
        y, ym = yield from layernorm(xn, total, col("l3g"), col("l3be"))
        tiles.give(xn, ym)
        done = yield from stt(xs, y, 0.5, xs, ALU.mult, ALU.add, [*ym, *x_ready[c]])
        tiles.give(y, [done])
        x_ready[c] = [done]

    n_marks = []

    def open_b():
        before = [q.mark() for q in (pe, act, dve, pool)]
        n_marks.extend([load_native(w1n, n1, before), load_native(w2n, n2, before), load_native(w3n, n3, before)])
        a = yield from func(ACT.Exp, neg_a[:, :], colv[:, COLS["m2A"]:COLS["m2A"] + 16], [])
        n_marks.append((yield from step(dve, lambda e: e.memset(ones[:, :], 1.0), before)))
        n_marks.append((yield from ts(neg_a[:, :], neg_a[:, :], -1.0, ALU.mult, [a])))
        for i in range(EXTRA):
            tiles.give(extra[:, i, :], before)

    def load_b():
        before = [q.mark() for q in (pe, act, dve, pool)]
        yield from load_split(w1r, w1, L1W_COLS, before, w1_marks)
        yield from load_split(w2r, w2, L2W_COLS, before, w2_marks)

    def open_c(k0, k1):
        yield when()
        before = [q.mark() for q in (pe, act, dve, pool)]
        for k in range(k0, k1):
            slots3.give(k, before)

    def softplus(z, bank, bias, after):
        (a, af), (m, mf) = yield from tiles.take(2)
        x = yield from func(ACT.Abs, a, psum[:, bank, :], [*after, *af], bias=bias)
        y = yield from ts(m, psum[:, bank, :], bias, ALU.add, [*after, x, *mf], 0.0, ALU.max)
        banks.give(bank, [x, y])
        x = yield from func(ACT.Exp, a, a, [x], scale=-1.0)
        return a, m, [x, y]

    tail_marks = {}
    gate_m, begun = Gate(3), set()

    def mamba1(c):
        xs = X[:, c * C:(c + 1) * C]
        while c % 2 and ("mamba1", c - 1) not in begun:
            yield
        yield from gate_m.enter()
        begun.add(("mamba1", c))
        xn, xm = yield from layernorm(xs, x_ready[c])
        later = c % 2 == 1
        while later and (1, c - 1) not in tail_marks:
            yield
        xc, sz, new_tails = [None, None], [None, None], []
        def convolved(blk):
            t, tf = yield from tiles.take()
            b, bf = yield from banks.take()
            w0_ = N1["in"] + blk * P
            z = yield from full_mm(psum[:, b, :], [(w1n[:, w0_:w0_ + P], xn, [*xm, *n_marks])], bf)
            v = psum[:, b, :]
            tail = yield from copy_act(tails[:, c, blk, 0:3], v[:, C - 3:C], [z])
            m = yield from ts(t, v, col("m1conv", 6 + blk), ALU.mult, [z, tail, *tf])
            for d in range(1, 4):
                w = col("m1conv", 2 * (3 - d) + blk)
                m = yield from stt(t[:, d:C], v[:, 0:C - d], w, t[:, d:C], ALU.mult, ALU.add, [m])
                if later:
                    m = yield from stt(t[:, 0:d], tails[:, c - 1, blk, 3 - d:3], w, t[:, 0:d], ALU.mult, ALU.add,
                                       [m, *tail_marks[1, c - 1]])
            banks.give(b, [tail, m])
            new_tails.append(tail)
            xc[blk] = (t, (yield from func(ACT.Silu, t, t, [m], bias=col("m1cb", blk))))

        def gating(blk):
            t, tf = yield from tiles.take()
            b, bf = yield from banks.take()
            w0_ = N1["in"] + (2 + blk) * P
            z = yield from full_mm(psum[:, b, :], [(w1n[:, w0_:w0_ + P], xn, [*xm, *n_marks])], bf)
            sz[blk] = (t, (yield from func(ACT.Silu, t, psum[:, b, :], [z, *tf])))
            banks.give(b, [sz[blk][1]])

        yield from together([convolved(0), convolved(1), gating(0), gating(1)])
        tail_marks[1, c] = new_tails
        tiles.give(xn, [pe.mark()])
        sp = []
        for o in range(2):
            b, bf = yield from banks.take()
            z = yield from full_mm(psum[:, b, :], [(w1n[:, N1["dt"] + k * 2 * P + o * P:N1["dt"] + k * 2 * P + (o + 1) * P], xc[k][0],
                                         [xc[k][1]]) for k in range(2)], bf)
            sp.append((yield from softplus(z, b, col("m1dtb", o), [z])))
        dt = []
        for o in range(2):
            a, m, marks = sp[o]
            x = yield from func(ACT.Ln, a, a, marks, bias=1.0)
            y = yield from tt(m, a, m, ALU.add, [x, *marks])
            y = yield from tt(m, m, xc[o][0], ALU.mult, [y])
            tiles.give(a, [y])
            dt.append((m, y))
        (b, bf), (bt, tf), (ct, cf) = (yield from banks.take()), (yield from tiles.take()), (yield from tiles.take())
        for k in range(2):
            for half in range(2):
                c0 = N1["x"] + k * 32 + half * 16
                z = yield from step(pe, lambda e, o=psum[32 * half:32 * half + 16, b, :], l=w1n[:, c0:c0 + 16], r=xc[k][0], k=k, h=half:
                          e.matmul(o, l, r, start=(k == 0), stop=(k == 1), tile_position=(0, 32 * h)), bf)
        m = yield from copy_act(bt[0:16, :], psum[0:16, b, :], [z, *tf])
        m = yield from tt(ct[0:16, :], psum[32:48, b, :], bt[0:16, :], ALU.mult, [m, *cf])
        tiles.give(bt, [m])
        banks.give(b, [m])
        (bs, fs), (bg, fg) = (yield from banks.take()), (yield from banks.take())
        s_ = yield from full_mm(psum[:, bs, :], [(ones[:, :], dt[o][0], [dt[o][1]]) for o in range(2)], fs)
        g_ = yield from product(psum[:, bg, :], ones[0:16, :], ct[0:16, :], [m, *fg])
        for t, _ in dt:
            tiles.give(t, [s_])
        g, gf = yield from tiles.take()
        tiles.give(ct, [g_])
        m = yield from copy_act(g, psum[:, bg, :], [g_, *gf])
        banks.give(bg, [m])
        m = yield from tt(g, psum[:, bs, :], g, ALU.mult, [m, s_])
        banks.give(bs, [m])
        ys = []
        for k in range(2):
            t = xc[k][0]
            y = yield from stt(t, t, col("m1D", k), g, ALU.mult, ALU.add, [m, z])
            y = yield from tt(t, t, sz[k][0], ALU.mult, [y, sz[k][1]])
            tiles.give(sz[k][0], [y])
            ys.append((w1n[:, N1["o"] + k * P:N1["o"] + (k + 1) * P], t, [y]))
        tiles.give(g, [y])
        b, bf = yield from banks.take()
        z = yield from full_mm(psum[:, b, :], ys, bf)
        for k in range(2):
            tiles.give(xc[k][0], [z])
        done = yield from tt(xs, psum[:, b, :], xs, ALU.add, [z])
        banks.give(b, [done])
        x_ready[c] = [done]
        gate_m.leave()

    state_marks = {}
    STATES = 5

    def mamba2(c):
        xs = X[:, c * C:(c + 1) * C]
        while c % 2 and ("mamba2", c - 1) not in begun:
            yield
        yield from gate_m.enter()
        begun.add(("mamba2", c))
        src, sm = yield from layernorm(xs, x_ready[c])
        hn, hm = yield from layernorm(src, sm, col("n1g"), col("n1b"))
        later = c % 2 == 1
        while later and (2, c - 1) not in tail_marks:
            yield
        b, bf = yield from banks.take()
        z = yield from full_mm(psum[:, b, :], [(w2n[:, 0:P], hn, [*hm, *n_marks])], bf)
        xc, tf = yield from tiles.take()
        v = psum[:, b, :]
        tail = yield from copy_act(tails[:, c, 0, 3:4], v[:, C - 1:C], [z])
        m = yield from ts(xc, v, col("m2conv", 1), ALU.mult, [z, tail, *tf])
        m = yield from stt(xc[:, 1:C], v[:, 0:C - 1], col("m2conv", 0), xc[:, 1:C], ALU.mult, ALU.add, [m])
        if later:
            m = yield from stt(xc[:, 0:1], tails[:, c - 1, 0, 3:4], col("m2conv", 0), xc[:, 0:1], ALU.mult, ALU.add,
                    [m, tail_marks[2, c - 1]])
        banks.give(b, [tail, m])
        tail_marks[2, c] = tail
        xm = yield from func(ACT.Silu, xc, xc, [m], bias=col("m2cb"))
        b, bf = yield from banks.take()
        z = yield from full_mm(psum[:, b, :], [(w2n[:, P:2 * P], hn, hm)], bf)
        tiles.give(hn, [z])
        sz, zf = yield from tiles.take()
        szm = yield from func(ACT.Silu, sz, psum[:, b, :], [z, *zf])
        banks.give(b, [szm])
        b, bf = yield from banks.take()
        z = yield from product(psum[0:64, b, :], w2n[:, N2["xdt"]:N2["xdt"] + 64], xc, [xm, *bf])
        d64, df = yield from tiles.take()
        dm = yield from copy_act(d64[0:64, :], psum[0:64, b, :], [z, *df])
        banks.give(b, [dm])
        b, bf = yield from banks.take()
        z = yield from product(psum[0:96, b, :], w2n[:, N2["xbc"]:N2["xbc"] + 96], xc, [xm, *bf])
        (bc, f1), (rest, f2) = yield from tiles.take(2)
        bcb = bc.bitcast(BF16)[:, 0:C]
        m = yield from copy_act(bcb[0:96, :], psum[0:96, b, :], [z, *f1])
        m = yield from tt(rest[0:96, :], psum[0:96, b, :], bcb[0:96, :], ALU.subtract, [m, *f2])
        banks.give(b, [m])
        for r0 in (32, 64):
            m1 = yield from copy_act(bcb[r0:r0 + 32, :], rest[r0:r0 + 32, :], [m])
        m = yield from tt(rest[64:96, :], rest[64:96, :], bcb[64:96, :], ALU.subtract, [m1])
        bcm = yield from copy_act(bcb[64:96, :], rest[64:96, :], [m])
        tiles.give(rest, [bcm])
        b, bf = yield from banks.take()
        z = yield from product(psum[:, b, :], w2n[0:64, N2["dt"]:N2["dt"] + P], d64[0:64, :], [dm, *bf])
        tiles.give(d64, [z])
        a, dl, marks = yield from softplus(z, b, col("m2dtb"), [z])
        x = yield from func(ACT.Ln, a, a, marks, bias=1.0)
        dlm = yield from tt(dl, a, dl, ALU.add, [x, *marks])
        um = yield from tt(a, dl, xc, ALU.mult, [dlm, xm])
        u = a
        by, yf = yield from banks.take()
        added = []

        def state(n):
            while later and (c - 1, n) not in state_marks:
                yield
            (da, g1), (db, g2) = yield from tiles.take(2)
            m1 = yield from func(ACT.Exp, da, dl, [dlm, *g1], scale=neg_a[:, n:n + 1])
            bb, f1 = yield from banks.take()
            zb = yield from product(psum[:, bb, :], pickb[:, n:n + 1].broadcast_to([96, P]), bcb[0:96, :], [bcm, *f1])
            m2 = yield from tt(db, psum[:, bb, :], u, ALU.mult, [zb, um, *g2])
            banks.give(bb, [m2])
            start, wait = (states[:, c // 2, n:n + 1], [state_marks[c - 1, n]]) if later else (0.0, [])
            h = yield from step(dve, lambda e: e.tensor_tensor_scan(da, da, db, start, ALU.mult, ALU.add),
                                [m1, m2, *wait], 0.62)
            if not later:
                state_marks[c, n] = yield from step(pool, lambda e: e.tensor_copy(states[:, c // 2, n:n + 1],
                                                                                  da[:, C - 1:C]), [h])
            bb, f1 = yield from banks.take()
            zc = yield from product(psum[:, bb, :], pickb[:, NS + n:NS + n + 1].broadcast_to([96, P]), bcb[0:96, :],
                                    [bcm, *f1])
            m = yield from copy_act(db, psum[:, bb, :], [zc, h])
            banks.give(bb, [m])
            m = yield from tt(db, db, da, ALU.mult, [m, h], pool)
            tiles.give(da, [m])
            yield when(m, *yf)
            added.append(mm(psum[:, by, :], ident, db, not added, len(added) == NS - 1, [m, *yf], True))
            tiles.give(db, [added[-1]])

        yield from together([state(n) for n in range(NS)], STATES)
        y, (m1, m2, zc) = added[-1], [act.mark(), dve.mark(), pe.mark()]
        tiles.give(bc, [zc])
        tiles.give(dl, [m1])
        tiles.give(u, [m2])
        m = yield from stt(xc, xc, col("m2D"), psum[:, by, :], ALU.mult, ALU.add, [y])
        banks.give(by, [m])
        m = yield from tt(xc, xc, sz, ALU.mult, [m, szm])
        b, bf = yield from banks.take()
        z = yield from full_mm(psum[:, b, :], [(w2n[:, N2["o"]:N2["o"] + P], xc, [m])], bf)
        tiles.give(xc, [z])
        m = yield from copy_act(sz, psum[:, b, :], [z, m])
        banks.give(b, [m])
        yn, ym = yield from layernorm(sz, [m], col("mg"), col("mb"))
        tiles.give(sz, ym)
        sm = [(yield from tt(src, src, yn, ALU.add, [*ym, *sm]))]
        tiles.give(yn, sm)
        fn, fm = yield from layernorm(src, sm, col("n2g"), col("n2b"))
        hid = []
        for o in range(4):
            b, bf = yield from banks.take()
            z = yield from full_mm(psum[:, b, :], [(w2n[:, N2["f1"] + o * P:N2["f1"] + (o + 1) * P], fn, fm)], bf)
            t, tf = yield from tiles.take()
            m = yield from func(ACT.Copy, t, psum[:, b, :], [z, *tf], scale=0.01)
            m = yield from tt(t, psum[:, b, :], t, ALU.max, [m])
            banks.give(b, [m])
            hid.append((w2n[:, N2["f2"] + o * P:N2["f2"] + (o + 1) * P], t, [m]))
        tiles.give(fn, [z])
        b, bf = yield from banks.take()
        z = yield from full_mm(psum[:, b, :], hid, bf)
        for _, t, _ in hid:
            tiles.give(t, [z])
        sm = [(yield from tt(src, psum[:, b, :], src, ALU.add, [z, *sm]))]
        banks.give(b, sm)
        fn, fm = yield from layernorm(src, sm, col("n3g"), col("n3b"))
        b, bf = yield from banks.take()
        z = yield from full_mm(psum[:, b, :], [(w2n[:, N2["fe"]:N2["fe"] + P], fn, fm)], bf)
        tiles.give(fn, [z])
        m = yield from stt(src, psum[:, b, :], col("feb"), src, ALU.add, ALU.add, [z, *sm])
        banks.give(b, [m])
        done = yield from tt(xs, xs, src, ALU.add, [m])
        tiles.give(src, [done])
        x_ready[c] = [done]
        gate_m.leave()

    gate_l = Gate(1)

    def positive(bank, z):
        t, tf = yield from tiles.take()
        m = yield from ts(t, psum[:, bank, :], 0.0, ALU.min, [z, *tf])
        m = yield from func(ACT.Exp, t, t, [m])
        m = yield from stt(t, psum[:, bank, :], 0.0, t, ALU.max, ALU.add, [m])
        banks.give(bank, [m])
        return t, m

    def linear_attention(b_):
        yield from gate_l.enter()
        xn = [None, None]

        def norm(half):
            c = 2 * b_ + half
            xn[half] = yield from layernorm(X[:, c * C:(c + 1) * C], x_ready[c])

        yield from together([norm(0), norm(1)])
        (bkv, fkv), (bks, fks) = (yield from banks.take()), (yield from banks.take())
        for half in range(2):
            x_, xm = xn[half]
            toks = []
            for name in ("k", "v"):
                b, bf = yield from banks.take()
                yield when(*xm, *bf)
                for t in range(TPC):
                    z = mm(psum[:, b, t * TILE:(t + 1) * TILE], x_[:, t * TILE:(t + 1) * TILE],
                           w3n[:, N3[name]:N3[name] + P], True, True, [*xm, *bf, *n_marks], t == TPC - 1)
                if name == "k":
                    toks.append((yield from positive(b, z)))
                else:
                    t_, tf = yield from tiles.take()
                    m = yield from copy_act(t_, psum[:, b, :], [z, *tf])
                    banks.give(b, [m])
                    toks.append((t_, m))
            (kt, km), (vt, vm) = toks
            yield when(km, vm, *fkv, *fks)
            for t in range(TPC):
                first, last = half == 0 and t == 0, half == 1 and t == TPC - 1
                sl = slice(t * TILE, (t + 1) * TILE)
                mm(psum[:, bkv, 0:P], kt[:, sl], vt[:, sl], first, last, [km, vm, *fkv])
                z = mm(psum[:, bks, 0:P], kt[:, sl], ones[:, :], first, last, fks, t == TPC - 1)
            tiles.give(kt, [z])
            tiles.give(vt, [z])
        st, sf = yield from tiles.take()
        m = yield from tt(st[:, 0:P], psum[:, bkv, 0:P], heads, ALU.mult, [z, *sf])
        m = yield from tt(st[:, P:2 * P], psum[:, bks, 0:P], heads, ALU.mult, [z, m])
        banks.give(bkv, [m])
        banks.give(bks, [m])
        outs = []
        for half in range(2):
            x_, xm = xn[half]
            b, bf = yield from banks.take()
            z = yield from full_mm(psum[:, b, :], [(w3n[:, N3["q"]:N3["q"] + P], x_, xm)], bf)
            q, qm = yield from positive(b, z)
            (bn, fn), (bd, fd) = (yield from banks.take()), (yield from banks.take())
            zn = yield from full_mm(psum[:, bn, :], [(st[:, 0:P], q, [qm, m])], fn)
            zd = yield from full_mm(psum[:, bd, :], [(st[:, P:2 * P], q, [])], fd)
            d = yield from ts(q, psum[:, bd, :], 1e-6, ALU.max, [zd, zn])
            banks.give(bd, [d])
            d = yield from reciprocal(q, q, [d])
            d = yield from tt(q, psum[:, bn, :], q, ALU.mult, [d, zn])
            banks.give(bn, [d])
            loc, lf = yield from tiles.take()
            l_ = yield from ts(loc, x_, col("c3w", 1), ALU.mult, [*xm, *lf], col("c3b"), ALU.add)
            l_ = yield from stt(loc[:, 1:C], x_[:, 0:C - 1], col("c3w", 0), loc[:, 1:C], ALU.mult, ALU.add, [l_])
            l_ = yield from stt(loc[:, 0:C - 1], x_[:, 1:C], col("c3w", 2), loc[:, 0:C - 1], ALU.mult, ALU.add, [l_])
            other, om = xn[1 - half]
            if half:
                l_ = yield from stt(loc[:, 0:1], other[:, C - 1:C], col("c3w", 0), loc[:, 0:1], ALU.mult, ALU.add, [l_, *om])
            else:
                l_ = yield from stt(loc[:, C - 1:C], other[:, 0:1], col("c3w", 2), loc[:, C - 1:C], ALU.mult, ALU.add, [l_, *om])
            l_ = yield from tt(loc, loc, q, ALU.add, [l_, d])
            tiles.give(q, [l_])
            outs.append((loc, l_))
        tiles.give(st, [zd])
        for half in range(2):
            tiles.give(xn[half][0], [outs[1][1], z])
        for half in range(2):
            loc, l_ = outs[half]
            c = 2 * b_ + half
            xs = X[:, c * C:(c + 1) * C]
            b, bf = yield from banks.take()
            z = yield from full_mm(psum[:, b, :], [(w3n[:, N3["p"]:N3["p"] + P], loc, [l_])], bf)
            tiles.give(loc, [z])
            done = yield from stt(xs, psum[:, b, :], col("bp"), xs, ALU.add, ALU.add, [z])
            banks.give(b, [done])
            x_ready[c] = [done]
        gate_l.leave()


    jobs = []
    jobs.append(("w0", lambda: load_split(w0r, w0, L0W_COLS, [], w0_marks), []))
    for c in range(NC_):
        jobs.append((("ffn0", c), lambda c=c: ffn0(c), []))
    jobs.append(("attn_setup", attn_setup, []))
    for b in range(NB):
        jobs.append((("attn0", b), lambda b=b: attention(b), ["attn_setup", ("ffn0", 2 * b), ("ffn0", 2 * b + 1)]))
    for c in range(NC_):
        jobs.append((("ffn0b", c), lambda c=c: ffn0(c), [("attn0", b) for b in range(NB)]))
    last = [("ffn0b", c) for c in range(NC_)]

    def stage(name, make, order=range(NC_), before=(), per=1):
        nonlocal last
        for i in order:
            deps = [last[c] for c in range(per * i, per * (i + 1))]
            jobs.append(((name, i), lambda i=i: make(i), [*deps, *before]))
        last = [(name, c // per) for c in range(NC_)]

    across = (0, 2, 4, 6, 1, 3, 5, 7)
    jobs.append(("load_b", load_b, [("attn0", b) for b in range(NB)]))
    jobs.append(("open_b", open_b, list(last)))
    stage("moe1", lambda c: moe1(c, c))
    stage("mamba1", mamba1, across, before=["open_b"])
    stage("moe1b", lambda c: moe1(c, NC_ + c))
    stage("moe2", lambda c: moe2(c, 2 * NC_ + c))
    stage("mamba2", mamba2, across)
    stage("moe2b", lambda c: moe2(c, 3 * NC_ + c))
    jobs.append(("open_c1", lambda: open_c(0, EARLY), [("moe1b", c) for c in range(NC_)]))
    jobs.append(("open_c2", lambda: open_c(EARLY, NEXP), list(last)))
    jobs.append(("stream3", lambda: stream3(4), ["open_c1"]))
    stage("moe3", lambda c: moe3(c, 4 * NC_ + c))
    stage("attn3", linear_attention, range(NB), per=2)
    jobs.append(("stream3b", lambda: stream3(5), ["stream3"]))
    stage("moe3b", lambda c: moe3(c, 5 * NC_ + c))
    run_jobs(jobs, 7)

    ends = [dma.do(out[:, c * C:(c + 1) * C], X[:, c * C:(c + 1) * C], x_ready[c]) for c in range(NC_)]

    with nc.Block() as block:
        @block.sync
        def _(eng):
            dma.replay(eng)
            for i, sem in enumerate(dma.sems):
                turns = (dma.n - i + len(dma.sems) - 1) // len(dma.sems)
                if turns > 0:
                    eng.wait_ge(sem, 16 * turns)

        @block.tensor
        def _(eng):
            pe.replay(eng)

        @block.scalar
        def _(eng):
            act.replay(eng)

        @block.vector
        def _(eng):
            dve.replay(eng)

        @block.gpsimd
        def _(eng):
            pool.replay(eng)


def kernel(**inputs):
    import numpy as np
    import concourse.bacc as bacc
    from concourse.bass_utils import run_bass_kernel_spmd

    g = {k: np.asarray(v) for k, v in inputs.items()}

    def lhs(w):
        o, i = w.shape
        k = -(-i // P)
        full = np.zeros((k * P, o), w.dtype)
        full[:i] = w.T
        return full.reshape(k, P, o).transpose(1, 0, 2).reshape(P, k * o)

    def side(*parts):
        return np.ascontiguousarray(np.concatenate(parts, axis=1))

    def columns(v):
        return np.asarray(v).reshape(-1, P).T

    swap = np.arange(P) ^ 1
    wq, wk, wv = np.split(g["L0_attn_w_qkv"], 3)
    bq, bk, bv = np.split(g["L0_attn_b_qkv"], 3)
    packed = {
        "x_t": g["L0_attn_x"].reshape(T, P).T,
        "w0": side(lhs(g["L0_ffn_w1_w"]), lhs(g["L0_ffn_w2_w"]), lhs(g["L0_ffn_h1_w"]), lhs(g["L0_ffn_h2_w"]),
                   lhs(g["L0_ffn_w3_w"])),
        "w1": side(*[g[f"L1_ffn_w{k}"][e] for e in range(E8) for k in (1, 2, 3)]),
        "w2": side(*[g[f"L2_ffn_w{k}"][e] for e in range(E8) for k in (1, 2)],
                   g["L2_ffn_shared_gate_up"], g["L2_ffn_shared_down"]),
        "w3": np.stack([side(lhs(g["L3_ffn_W1"][e]), lhs(g["L3_ffn_W2"][e])) for e in range(E8)]),
        "n0": side(lhs(wq), lhs(wq[swap]), lhs(wk), lhs(wk[swap]), lhs(wv), lhs(g["L0_attn_w_out"])),
        "n1": side(lhs(g["L1_attn_in_proj_w"]), lhs(g["L1_attn_dt_proj_w"]), lhs(g["L1_attn_x_proj_w"]),
                   lhs(g["L1_attn_out_proj_w"])),
        "n2": side(lhs(g["L2_attn_in_proj_w"]), lhs(g["L2_attn_x_proj_w"][:64]),
                   *[lhs(g["L2_attn_x_proj_w"][64:])] * 3, lhs(g["L2_attn_dt_proj_w"]),
                   lhs(g["L2_attn_out_proj_w"]), lhs(g["L2_attn_ffn_w1"]), lhs(g["L2_attn_ffn_w2"]),
                   lhs(g["L2_attn_fe_w"])),
        "n3": side(*[lhs(g[f"L3_attn_W{k}"]) for k in "qkvp"]),
        "rw": side(g["L1_ffn_gate_w"].T, g["L2_ffn_router_w"], g["L2_ffn_shared_gate_w"], g["L3_ffn_Wr"].T),
    }
    cols = {"s1": g["L0_ffn_w1_s"], "s2": g["L0_ffn_w2_s"], "h1s": g["L0_ffn_h1_s"], "h2s": g["L0_ffn_h2_s"],
            "w3s": g["L0_ffn_w3_s"], "bq": bq, "bqs": bq[swap], "bk": bk, "bks": bk[swap], "bo": g["L0_attn_b_out"],
            "l1b1": g["L1_ffn_b1"], "l1b2": g["L1_ffn_b2"], "l1b3": g["L1_ffn_b3"],
            "m1conv": g["L1_attn_conv_w"][:, 0, :].T, "m1cb": g["L1_attn_conv_b"], "m1dtb": g["L1_attn_dt_proj_b"],
            "m1D": g["L1_attn_D_param"], "m2conv": g["L2_attn_conv_w"].T, "m2cb": g["L2_attn_conv_b"],
            "m2dtb": g["L2_attn_dt_proj_b"], "m2D": g["L2_attn_Dp"], "m2A": g["L2_attn_A_log"].T,
            "mg": g["L2_attn_mnorm_g"], "mb": g["L2_attn_mnorm_b"], "n1g": g["L2_attn_n1_g"], "n1b": g["L2_attn_n1_b"],
            "n2g": g["L2_attn_n2_g"], "n2b": g["L2_attn_n2_b"], "n3g": g["L2_attn_n3_g"], "n3b": g["L2_attn_n3_b"],
            "feb": g["L2_attn_fe_b"], "c3w": g["L3_attn_conv_w"].T, "c3b": g["L3_attn_conv_b"], "bp": g["L3_attn_bp"],
            "l3b1": g["L3_ffn_b1"], "l3b2": g["L3_ffn_b2"], "l3g": g["L3_ffn_gamma"], "l3be": g["L3_ffn_beta"]}
    packed["cols"] = side(*[columns(np.ascontiguousarray(cols[k])) for k in COLS])
    f = np.float32
    packed["rows"] = np.concatenate([g["L1_ffn_gate_b"], g["L3_ffn_br"], np.arange(8, 0, -1).astype(f), bv])[None, :]
    i, j = np.arange(P)[:, None], np.arange(P)[None, :]
    band = np.arange(224)[None, :]
    num = (i % 32 < 8) & (band == 96 + 8 * (i // 32) + i % 32)
    den = (i % 32 == 8) & (band >= 96 + 8 * (i // 32)) & (band < 104 + 8 * (i // 32))
    packed["mats"] = side((i == j).astype(f), (i // HD == j // HD).astype(f), num.astype(f), den.astype(f),
                          ((i == j) - f(1 / P)).astype(f), np.where(j > i, f(NEG), f(0)), np.where(j < i, f(NEG), f(0)),
                          ((i % 32 == np.arange(32)) & (i < 96)).astype(f))
    dims = np.arange(0, HD, 2, dtype=f)
    inv = (f(1) / f(10000.0) ** (dims / f(HD))).astype(f)
    ang = np.arange(S, dtype=f)[:, None] * inv[None, :]
    feat = np.arange(P)
    cos, sin = np.cos(ang).astype(f)[:, feat % HD // 2].T, np.sin(ang).astype(f)[:, feat % HD // 2].T
    packed["rope"] = np.stack([cos, np.where(feat % 2, f(1), f(-1))[:, None] * sin], axis=1)

    packed["zero"] = np.zeros((1, S), f)

    nc = bacc.Bacc("TRN2", target_bir_lowering=False, num_devices=1)
    arrays, args = {}, {}
    for name, a in packed.items():
        a = np.ascontiguousarray(a)
        arrays[f"in_{name}"] = a
        args[name] = nc.dram_tensor(f"in_{name}", a.shape, F32, kind="ExternalInput").ap()
    args["rows"] = args["rows"].broadcast_to([P, NROWS])
    args["out"] = nc.dram_tensor("out_x", (P, T), F32, kind="ExternalOutput").ap()
    build(nc, **args)
    r = run_bass_kernel_spmd(nc, [arrays], core_ids=[0])
    return np.ascontiguousarray(r.results[0]["out_x"].T).reshape(NB, S, P)
```
